# Optimizing a Trainium2 kernel written in Bass

```python
import numpy as np
import jax
import jax.numpy as jnp

def _softmax(x, axis=-1):
    return jax.nn.softmax(x, axis=axis)

def _gelu(x):
    return jax.nn.gelu(x, approximate=True)

def _silu(x):
    return jax.nn.silu(x)

def _sigmoid(x):
    return jax.nn.sigmoid(x)

def _layernorm(x, axis=-1, eps=1e-05):
    m = jnp.mean(x, axis=axis, keepdims=True)
    v = jnp.var(x, axis=axis, keepdims=True)
    return (x - m) / jnp.sqrt(v + eps)

def _scatter_add(tgt, idx, src, axis=0):
    return tgt.at[idx].add(src)

def _segment_sum(src, seg, n):
    return jax.ops.segment_sum(src, seg, n)
kernel_name = 'mk_adj_resnorm_d1_adj_r2_824c2b'

def setup_inputs(seed: int=0):
    np.random.seed(seed)
    _w = jnp.asarray

    def _rec_inputs():
        import jax
        import jax.numpy as jnp
        _gk = jax.random.key(seed)
        x = -0.0005207 + 1.001 * jax.random.normal(jax.random.fold_in(_gk, 1), (4096, 256), jnp.float32)
        _w = (1.0 + jnp.arange(4096, dtype=jnp.float32)) ** (-0.5)
        _w = _w / _w.mean()
        _pij = jnp.clip(0.00390625 * _w[:, None] * _w[None, :], 0.0, 1.0)
        _a = jax.random.uniform(jax.random.fold_in(_gk, 2), (4096, 4096)) < _pij
        adj = _a.astype(jnp.int32)
        return (x, adj)
    x, adj = _rec_inputs()

    def _L0_gnn_setup():
        import jax, jax.numpy as jnp
        import numpy as np
        NEG_SLOPE = 0.2
        N, IN_DIM, OUT_DIM, N_HEADS = (2048, 256, 256, 4)
        D_K = OUT_DIM // N_HEADS
        key = jax.random.key(seed)
        k1, k2, k3, k4, k5 = jax.random.split(key, 5)
        H = jax.random.normal(k1, (N, IN_DIM), dtype=jnp.float32)
        A = jax.random.randint(k2, (N, N), 0, 2, dtype=jnp.int32)
        W = jax.random.normal(k3, (IN_DIM, OUT_DIM), dtype=jnp.float32) * (1.0 / np.sqrt(IN_DIM))
        a_l = jax.random.normal(k4, (N_HEADS, D_K), dtype=jnp.float32) * 0.1
        a_r = jax.random.normal(k5, (N_HEADS, D_K), dtype=jnp.float32) * 0.1
        return {'H': H, 'A': A, 'W': W, 'a_l': a_l, 'a_r': a_r}
    _L0_gnn_all = _L0_gnn_setup()
    _L0_gnn_in = {k: v for k, v in _L0_gnn_all.items() if k in ('W', 'a_l', 'a_r')}
    del _L0_gnn_all
    return {'x': x, 'adj': adj, 'L0_gnn_W': _L0_gnn_in['W'], 'L0_gnn_a_l': _L0_gnn_in['a_l'], 'L0_gnn_a_r': _L0_gnn_in['a_r']}

def reference(x, adj, L0_gnn_W, L0_gnn_a_l, L0_gnn_a_r):
    import jax
    import jax.numpy as jnp

    def _L0_gnn_ref(H, A, W, a_l, a_r):
        import jax, jax.numpy as jnp
        import numpy as np
        NEG_SLOPE = 0.2
        N, IN_DIM, OUT_DIM, N_HEADS = (2048, 256, 256, 4)
        D_K = OUT_DIM // N_HEADS
        n = H.shape[0]
        mask = A + jnp.eye(n, dtype=A.dtype) > 0
        Wh = (H @ W).reshape(n, N_HEADS, D_K)
        sl = jnp.einsum('nhd,hd->nh', Wh, a_l)
        sr = jnp.einsum('nhd,hd->nh', Wh, a_r)
        e = jax.nn.leaky_relu(sl[:, :, None] + sr.T[None, :, :], negative_slope=NEG_SLOPE)
        e = jnp.where(mask[:, None, :], e, -jnp.inf)
        alpha = jnp.nan_to_num(jax.nn.softmax(e, axis=2), nan=0.0)
        out = jnp.einsum('nhm,mhd->nhd', alpha, Wh).reshape(n, OUT_DIM)
        return jax.nn.elu(out)
    x = _layernorm(x + _L0_gnn_ref(x, adj, L0_gnn_W, L0_gnn_a_l, L0_gnn_a_r), axis=-1)
    return x

_drawn_inputs = setup_inputs


def setup_inputs(seed=0):
    import zlib

    import numpy as np

    out = dict(_drawn_inputs(seed))
    spreads = {}
    factors = {}
    for name, (base, spread) in spreads.items():
        noise = np.random.default_rng([zlib.crc32(name.encode()), seed]).standard_normal(out[name].shape)
        drawn = base * np.exp(spread * noise) if base else spread * noise
        out[name] = jnp.asarray(drawn.astype(out[name].dtype))
    for name, factor in factors.items():
        out[name] = (out[name] * factor).astype(out[name].dtype)
    return out
```

```python
def graph_attention(nc, x, adj, w, a_l, a_r, sl_rows, out):
    from contextlib import ExitStack
    from concourse import mybir

    dt, ALU, ACT = mybir.dt, mybir.AluOpType, mybir.ActivationFunctionType
    AX = mybir.AxisListType
    F32, F16, I32, U32, U8, I8, F8 = dt.float32, dt.float16, dt.int32, dt.uint32, dt.uint8, dt.int8, dt.float8e4

    P = 128
    N, D = x.shape
    H, DK = a_l.shape
    SUB = 4
    BLK = SUB * P
    NB = N // BLK
    KT = D // P
    DK1 = DK + 1
    PW = 2 * DK1
    WX = D + 2 * H
    QB = 2
    NQ = NB // QB
    WORDS = QB * BLK
    ACT_SHARE = 5
    BIT = 0x20
    EDGE, CODE0 = 0x01010101, 0x40
    WIDE = 2.0 ** 13
    WIDE1 = 2.0 ** 14
    TINY = 1e-30
    EPS = 1e-5

    ctx = ExitStack()
    with ctx:
        def sb(name, shape, t):
            return ctx.enter_context(nc.sbuf_tensor(name, shape, t))

        def pb(name, shape, t):
            return ctx.enter_context(nc.psum_tensor(name, shape, t))

        def sem(name):
            return ctx.enter_context(nc.semaphore(name))

        ident = sb("ident", [P, P], F32)
        eye = sb("eye", [P, SUB, BLK], I32)
        ones = sb("ones", [2 * H, P], F32)
        half = sb("half", [P, SUB], F32)
        wext = sb("wext", [P, KT, WX], F32)
        slr = sb("slr", [P, NB, SUB, 2 * H], F32)
        nsr = sb("nsr", [P, NB, SUB, H], F32)
        bd = sb("bd", [P, 2, NB, SUB, H], F32)
        cn = sb("cn", [P, NB, SUB, H], F32)
        rmax = sb("rmax", [2 * H, NB + 1], F32)
        wmax = sb("wmax", [P, 2 * NB + 2], F32)
        top = sb("top", [2 * H, 2 * H + 1], F32)
        smax = sb("smax", [P, 2 * H], F32)
        wtop = sb("wtop", [P, 4], F32)
        parts = sb("parts", [P, NB, SUB, H, 2, PW], F16)
        room = sb("room", [P, NB * SUB * H * DK1], F32)
        wh = room[:, :].rearrange("p (m h d) -> p m h d", h=H, d=DK1)
        o_slb, o_sgn, o_neg, o_pos = 0, H * BLK, H * BLK + 2 * WORDS, H * BLK + 4 * WORDS
        slb = room[:, o_slb:o_sgn].rearrange("p (h n) -> p h n", h=H)
        sgn = room[:, o_sgn:o_neg].bitcast(U32).rearrange("p (s w) -> p s w", s=2)
        neg = room[:, o_neg:o_pos].bitcast(U32).rearrange("p (s w) -> p s w", s=2)
        pos = room[:, o_pos:o_pos + 2 * WORDS].bitcast(U32).rearrange("p (s w) -> p s w", s=2)
        adj_in = sb("adj_in", [P, 2, SUB, BLK], I32)
        adj_by = sb("adj_by", [P, 2, SUB * BLK], U8)
        mask = sb("mask", [P, 2, NB, BLK], U32)
        xin = sb("xin", [P, 2, SUB, D], F32)
        comb = sb("comb", [P, SUB, H, DK1], F32)
        td = sb("td", [P, SUB, PW], F32)
        ts = sb("ts", [P, SUB, PW], F32)
        den = sb("den", [P, 2, SUB, H], F32)
        y1 = sb("y1", [P, SUB, D], F32)
        y2 = sb("y2", [P, SUB, D], F32)
        stats = sb("stats", [P, SUB, 6], F32)
        mv = sb("mv", [P, SUB, 2], F32)
        var = sb("var", [P, SUB], F32)
        rstd = sb("rstd", [P, SUB], F32)
        shift = sb("shift", [P, SUB], F32)
        xt = sb("xt", [P, 2, KT, BLK], F32)
        rows = sb("rows", [2 * H, 2, BLK], F32)
        aw = sb("aw", [P, 2, D], F32)
        full = sb("full", [P, SUB, H, DK1], F32)
        full2 = sb("full2", [P, SUB, H, DK1], F32)
        t32 = sb("t32", [P, NB, SUB, H], F32)

        acc = pb("acc", [P, SUB, 512], F32)
        tb = pb("tb", [P, 2, 512], F32)
        rb = pb("rb", [P, 2, 512], F32)

        w_loaded, a_loaded = sem("w_loaded"), sem("a_loaded")
        x_loaded = [sem(f"x_loaded{i}") for i in range(2)]
        adj_loaded = [sem(f"adj_loaded{i}") for i in range(2)]
        rows_stored = [sem(f"rows_stored{i}") for i in range(2)]
        sl_loaded = [sem(f"sl_loaded{h}") for h in range(H)]
        res_loaded, out_stored = sem("res_loaded"), sem("out_stored")
        consts_ready, wext_ready = sem("consts_ready"), sem("wext_ready")
        x_turned, xt_act, xt_dve = sem("x_turned"), sem("xt_act"), sem("xt_dve")
        wh_done, wh_copied, slr_copied = sem("wh_done"), sem("wh_copied"), sem("slr_copied")
        rows_turned, rows_copied, top_ready = sem("rows_turned"), sem("rows_copied"), sem("top_ready")
        wmax_ready, wmax_turned, smax_done, exps_ready = sem("wmax_ready"), sem("wmax_turned"), sem("smax_done"), sem("exps_ready")
        args_ready, cn_ready = sem("args_ready"), sem("cn_ready")
        full_ready, head_ready, parts_ready = sem("full_ready"), sem("head_ready"), sem("parts_ready")
        diag_fixed, bytes_ready, mask_turned, mask_ready = sem("diag_fixed"), sem("bytes_ready"), sem("mask_turned"), sem("mask_ready")
        cmp_act, cmp_dve, pair_ready, quarter_done = sem("cmp_act"), sem("cmp_dve"), sem("pair_ready"), sem("quarter_done")
        quarter_begun = sem("quarter_begun")
        acc_done, d_scaled, acc_free = sem("acc_done"), sem("d_scaled"), sem("acc_free")
        neg_part, exp_part, sum_done, var_ready = sem("neg_part"), sem("exp_part"), sem("sum_done"), sem("var_ready")
        rstd_ready, shift_ready, norm_done = sem("rstd_ready"), sem("shift_ready"), sem("norm_done")
        dve_order, act_order, pool_order = sem("dve_order"), sem("act_order"), sem("pool_order")

        CASTS = {1: 0, 2: 1, 4: 2, 5: 3, 7: 4, 8: 5, 10: 6, 11: 7}
        assert NB == 8 and NQ == 4 and H == 4

        def count_diag(c, q):
            return (c * (NB - 1) + (q + NB)) >> 3

        block = ctx.enter_context(nc.Block())

        @block.sync
        def _(sp):
            def load_adj(c, q):
                if isinstance(c, int) and c == 0:
                    src = adj[0:BLK, q * BLK:(q + 1) * BLK]
                else:
                    src = adj.rearrange("(c r) m -> c r m", r=BLK)[c, :, q * BLK:(q + 1) * BLK]
                if not isinstance(c, int) or NB * c + q >= 2:
                    sp.wait_ge(bytes_ready, NB * c + (q - 1))
                sp.dma_start(adj_in[:, q % 2], src.rearrange("(p s) m -> p s m", s=SUB)).then_inc(adj_loaded[q % 2], 16)

            def load_sl(c, h):
                if not isinstance(c, int):
                    sp.wait_ge(cmp_act, 4 * H * (c - 1) + (4 * h + 4))
                    sp.wait_ge(cmp_dve, 4 * H * (c - 1) + (4 * h + 4))
                src = sl_rows.rearrange("h (c n) -> c h n", n=BLK)[c, h:h + 1, :]
                sp.dma_start(slb[:, h, :], src.to_broadcast([P, BLK])).then_inc(sl_loaded[h], 16)

            def load_res(c):
                src = x.rearrange("(c p s) d -> c p s d", p=P, s=SUB)[c]
                sp.dma_start(xin[:, 0], src).then_inc(res_loaded, 16)

            sp.dma_start(wext[:, :, 0:D], w.rearrange("(k p) d -> p k d", p=P)).then_inc(w_loaded, 16)
            for i, a in enumerate((a_l, a_r)):
                sp.dma_start(aw[:, i, :], a.rearrange("h d -> (h d)").unsqueeze(0).to_broadcast([P, D])).then_inc(a_loaded, 16)
            for q in range(NB + 1):
                if q < NB:
                    if q >= 2:
                        sp.wait_ge(x_turned, q - 1)
                    sp.dma_start(xin[:, q % 2], x[q * BLK:(q + 1) * BLK, :].rearrange("(p s) d -> p s d", s=SUB)).then_inc(x_loaded[q % 2], 16)
                    if q < 2:
                        load_adj(0, q)
                if q >= 1:
                    r = q - 1
                    sp.wait_ge(rows_copied, r + 1)
                    sp.dma_start(sl_rows[:, r * BLK:(r + 1) * BLK], rows[0:H, r % 2, :]).then_inc(rows_stored[r % 2], 16)
            for i in range(2):
                sp.wait_ge(rows_stored[i], 16 * (NB // 2))
            sp.wait_ge(parts_ready, NB)
            for h in range(H):
                load_sl(0, h)
            for q in range(2, NB):
                load_adj(0, q)
            load_res(0)
            with sp.Fori(0, NB - 1) as c:
                load_sl(c + 1, 0)
                for q in range(5):
                    load_adj(c + 1, q)
                load_sl(c + 1, 1)
                for q in range(5, 8):
                    load_adj(c + 1, q)
                load_sl(c + 1, 2)
                load_sl(c + 1, 3)
                sp.wait_ge(sum_done, c + 1)
                load_res(c + 1)

        @block.gpsimd
        def _(pool):
            links = [0]

            def link(ins):
                links[0] += 1
                ins.then_inc(pool_order, 1)
                pool.wait_ge(pool_order, links[0])

            link(nc.gpsimd.memset(ident[:], 0.0))
            nc.gpsimd.affine_select(out=ident[:], in_=ident[:], compare_op=ALU.not_equal, fill=1.0, base=0,
                                    pattern=[[-1, P]], channel_multiplier=1).then_inc(consts_ready, 1)
            nc.gpsimd.memset(ones[:], 1.0).then_inc(consts_ready, 1)
            nc.gpsimd.memset(wh[:, :, :, DK:DK1], 1.0).then_inc(consts_ready, 1)
            nc.gpsimd.memset(half[:], -0.5).then_inc(consts_ready, 1)
            pool.sem_inc(out_stored, 16)
            link(nc.gpsimd.memset(eye[:], 0))
            link(nc.gpsimd.affine_select(out=eye[:], in_=eye[:], compare_op=ALU.not_equal, fill=1.0, base=0,
                                         pattern=[[1, SUB], [-1, BLK]], channel_multiplier=SUB))

            def fix_diag(c):
                pool.wait_ge(adj_loaded[0], 16 * (4 * c + ((c >> 1) + 1)))
                if not isinstance(c, int):
                    pool.wait_ge(adj_loaded[1], 16 * (4 * c + ((c + 1) >> 1)))
                slot = adj_in[:, c & 1]
                nc.gpsimd.tensor_tensor(slot, slot, eye[:], ALU.add).then_inc(diag_fixed, 1)

            def inverse_root(c):
                pool.wait_ge(var_ready, c + 1)
                nc.gpsimd.tensor_tensor(rstd[:], var[:], half[:], ALU.pow).then_inc(rstd_ready, 1)

            fix_diag(0)
            with pool.Fori(0, NB - 1) as c:
                fix_diag(c + 1)
                inverse_root(c)
            inverse_root(NB - 1)

        @block.tensor
        def _(pe):
            def turn_mask(c, q):
                pe.wait_ge(bytes_ready, NB * c + (q + 1))
                if not isinstance(c, int) or NB * c + q >= 2:
                    pe.wait_ge(mask_ready, NB * c + (q - 1))
                by = adj_by[:, q % 2, :].bitcast(F32).rearrange("p (s w) -> p s w", s=SUB)
                for s in range(SUB):
                    last = nc.tensor.transpose(tb[:, q % 2, s * P:(s + 1) * P], by[:, s, :], ident[:])
                last.then_inc(mask_turned, 1)

            def unit(c, h, prep):
                u = H * c + h
                for k in range(NQ):
                    t = NQ * (h - 1) + k
                    if prep and h > 0 and t in CASTS:
                        turn_mask(c + 1, CASTS[t])
                    pe.wait_ge(pair_ready, NQ * u + (k + 1))
                    by = [m[:, k % 2, :].bitcast(F8).rearrange("p (q s j b) -> p q s j b", q=QB, s=SUB, b=SUB)
                          for m in (pos, neg)]
                    if k == 0 and (not isinstance(c, int) or u >= 1):
                        pe.wait_ge(acc_free, u)
                    pe.sem_inc(quarter_begun, 1)
                    for s in range(SUB):
                        for q in range(QB):
                            for b in range(SUB):
                                for i in range(2):
                                    first = k == 0 and q == 0 and b == 0
                                    final = k == NQ - 1 and q == QB - 1 and b == SUB - 1
                                    last = nc.tensor.matmul(acc[:, s, i * PW:(i + 1) * PW], by[i][:, q, s, :, b],
                                                            parts[:, QB * k + q, b, h, i, :],
                                                            start=first and i == 0, stop=final, skip_group_check=True)
                        if k == NQ - 1 and s < SUB - 1:
                            last.then_inc(acc_done, 1)
                    last.then_inc(quarter_done, 1)

            pe.wait_ge(consts_ready, 4)
            for q in range(NB):
                pe.wait_ge(x_loaded[q % 2], 16 * (q // 2 + 1))
                if q >= 1:
                    pe.wait_ge(xt_act, q)
                    pe.wait_ge(xt_dve, q)
                for kk in range(KT):
                    for s in range(SUB):
                        last = nc.tensor.transpose(tb[:, kk, s * P:(s + 1) * P], xin[:, q % 2, s, kk * P:(kk + 1) * P], ident[:])
                last.then_inc(x_turned, 1)
                pe.wait_ge(xt_act, q + 1)
                pe.wait_ge(xt_dve, q + 1)
                if q == 0:
                    pe.wait_ge(wext_ready, 1)
                else:
                    pe.wait_ge(wh_copied, q)
                    pe.wait_ge(slr_copied, q)
                for s in range(SUB):
                    for kk in range(KT):
                        last = nc.tensor.matmul(acc[:, s, 0:WX], xt[:, q % 2, kk, s * P:(s + 1) * P], wext[:, kk, :],
                                                start=kk == 0, stop=kk == KT - 1)
                last.then_inc(wh_done, 1)
                pe.wait_ge(slr_copied, q + 1)
                if q >= 2:
                    pe.wait_ge(rows_copied, q - 1)
                for s in range(SUB):
                    last = nc.tensor.transpose(rb[0:2 * H, q % 2, s * P:(s + 1) * P], slr[:, q, s, :], ident[:])
                last.then_inc(rows_turned, 1)
            pe.wait_ge(wmax_ready, 1)
            pe.wait_ge(rows_copied, NB)
            nc.tensor.transpose(rb[0:1, 1, 0:P], wmax[:, 2 * NB:2 * NB + 1], ident[:]).then_inc(wmax_turned, 1)
            pe.wait_ge(top_ready, 1)
            nc.tensor.matmul(rb[:, 0, 0:2 * H], ones[:, :], top[:, 0:2 * H], start=True, stop=True)
            nc.tensor.matmul(rb[:, 0, 2 * H:2 * H + 1], ones[0:1, :], top[0:1, 2 * H:2 * H + 1], start=False, stop=True,
                             skip_group_check=True).then_inc(smax_done, 1)
            for q in range(NB):
                turn_mask(0, q)
            pe.wait_ge(parts_ready, NB)
            unit(0, 0, False)
            with pe.Fori(0, NB - 1) as c:
                for h in range(1, H):
                    unit(c, h, True)
                unit(c + 1, 0, False)
            for h in range(1, H):
                unit(NB - 1, h, False)

        @block.scalar
        def _(act):
            def compare(c, h, k):
                g = NQ * (H * c + h) + k
                if k == 0:
                    act.wait_ge(sl_loaded[h], 16 * c + 16)
                if not isinstance(c, int) or g >= 2:
                    act.wait_ge(pair_ready, g - 1)
                to = sgn[:, k % 2, :].bitcast(I8).rearrange("p (q n b) -> p q n b", q=QB, b=SUB)
                for i in range(ACT_SHARE):
                    q, b = i // SUB, i % SUB
                    last = nc.scalar.activation(to[:, q, :, b], slb[:, h, :], ACT.Sign,
                                                bias=slr[:, QB * k + q, b, H + h:H + h + 1])
                last.then_inc(cmp_act, 1)

            def scale_d(c, h):
                u = H * c + h
                if not isinstance(c, int) or u >= 1:
                    act.wait_ge(acc_free, u)
                for s in range(SUB):
                    if s < SUB - 1:
                        act.wait_ge(acc_done, (SUB - 1) * u + (s + 1))
                    else:
                        act.wait_ge(quarter_done, NQ * u + NQ)
                    last = nc.scalar.activation(td[:, s, :], acc[:, s, PW:2 * PW], ACT.Copy,
                                                scale=cn[:, c, s, h:h + 1])
                last.then_inc(d_scaled, 1)

            def exp_negative(c):
                act.wait_ge(neg_part, c + 1)
                nc.scalar.activation(y2[:], y2[:], ACT.Exp).then_inc(exp_part, 1)

            def normalize(c):
                act.wait_ge(shift_ready, c + 1)
                for s in range(SUB):
                    last = nc.scalar.activation(y2[:, s, :], y1[:, s, :], ACT.Identity, bias=shift[:, s:s + 1],
                                                scale=rstd[:, s:s + 1])
                last.then_inc(norm_done, 1)
                act.wait_ge(norm_done, c + 1)
                act.dma_start(out.rearrange("(c p s) d -> c p s d", p=P, s=SUB)[c], y2[:]).then_inc(out_stored, 16)

            for q in range(NB):
                act.wait_ge(x_turned, q + 1)
                if q >= 2:
                    act.wait_ge(wh_done, q - 1)
                nc.scalar.copy(xt[:, q % 2, 0, :], tb[:, 0, :]).then_inc(xt_act, 1)
                act.wait_ge(slr_copied, q + 1)
                nc.scalar.copy(wh[:, SUB * q:SUB * (q + 1), :, 0:DK],
                               acc[:, :, 0:D].rearrange("p s (h d) -> p s h d", h=H)).then_inc(wh_copied, 1)
            act.wait_ge(args_ready, 1)
            nc.scalar.activation(bd[:, 0], t32[:], ACT.Exp)
            nc.scalar.activation(bd[:, 1], t32[:], ACT.Exp, scale=0.2).then_inc(exps_ready, 1)
            act.wait_ge(args_ready, 2)
            nc.scalar.activation(cn[:], cn[:], ACT.Exp, scale=-0.8).then_inc(cn_ready, 1)
            for q in range(NB):
                for i, f in enumerate((full, full2)):
                    act.wait_ge(full_ready, 2 * q + i + 1)
                    nc.scalar.copy(parts[:, q, :, :, i, 0:DK1], f[:]).then_inc(head_ready, 1)

            act.wait_ge(cn_ready, 1)
            for k in range(NQ):
                compare(0, 0, k)
            with act.Fori(0, NB - 1) as c:
                for h in range(1, H):
                    for k in range(NQ):
                        compare(c, h, k)
                        if k == 0:
                            scale_d(c, h - 1)
                for k in range(NQ):
                    compare(c + 1, 0, k)
                    if k == 0:
                        scale_d(c, H - 1)
                    if k == 1:
                        exp_negative(c)
                normalize(c)
            for h in range(1, H):
                for k in range(NQ):
                    compare(NB - 1, h, k)
                    if k == 0:
                        scale_d(NB - 1, h - 1)
            scale_d(NB - 1, H - 1)
            exp_negative(NB - 1)
            normalize(NB - 1)
            act.wait_ge(out_stored, 16 * NB + 16)

        @block.vector
        def _(dve):
            links = [0]

            def link(ins):
                links[0] += 1
                ins.then_inc(dve_order, 1)
                dve.wait_ge(dve_order, links[0])

            def cast_adj(c, q):
                dve.wait_ge(adj_loaded[q % 2], 16 * (4 * c + (q // 2 + 1)))
                dve.wait_ge(diag_fixed, count_diag(c, q))
                if not isinstance(c, int) or NB * c + q >= 2:
                    dve.wait_ge(mask_turned, NB * c + (q - 1))
                nc.vector.tensor_scalar(adj_by[:, q % 2, :], adj_in[:, q % 2].rearrange("p s m -> p (s m)"), 0.0, float(CODE0),
                                        ALU.is_gt, ALU.add).then_inc(bytes_ready, 1)

            def take_mask(c, q):
                dve.wait_ge(mask_turned, NB * c + (q + 1))
                nc.vector.tensor_scalar(mask[:, c & 1, q, :], tb[:, q % 2, :].bitcast(U32), EDGE, 5,
                                        ALU.bitwise_and, ALU.logical_shift_left).then_inc(mask_ready, 1)

            def compare(c, h, k):
                if k == 0:
                    dve.wait_ge(sl_loaded[h], 16 * c + 16)
                to = sgn[:, k % 2, :].bitcast(U8).rearrange("p (q n b) -> p q n b", q=QB, b=SUB)
                for i in range(ACT_SHARE, QB * SUB):
                    q, b = i // SUB, i % SUB
                    last = nc.vector.tensor_scalar(to[:, q, :, b], slb[:, h, :], nsr[:, QB * k + q, b, h:h + 1],
                                                   float(BIT), ALU.is_le, ALU.mult)
                last.then_inc(cmp_dve, 1)

            def pair(c, h, k):
                g = NQ * (H * c + h) + k
                dve.wait_ge(cmp_act, g + 1)
                dve.wait_ge(cmp_dve, g + 1)
                dve.wait_ge(mask_ready, NB * c + QB * (k + 1))
                if not isinstance(c, int) or g >= 2:
                    dve.wait_ge(quarter_done, g - 1)
                m = mask[:, c & 1, QB * k:QB * (k + 1), :].rearrange("p q n -> p (q n)")
                nc.vector.tensor_tensor(neg[:, k % 2, :], sgn[:, k % 2, :], m, ALU.bitwise_and)
                nc.vector.scalar_tensor_tensor(out=pos[:, k % 2, :], in0=sgn[:, k % 2, :], scalar=BIT * EDGE, in1=m,
                                               op0=ALU.bitwise_xor, op1=ALU.bitwise_and).then_inc(pair_ready, 1)

            def add_sums(c, h):
                u = H * c + h
                dve.wait_ge(d_scaled, u + 1)
                nc.vector.tensor_tensor(ts[:], acc[:, :, 0:PW], td[:], ALU.add).then_inc(acc_free, 1)
                dve.wait_ge(acc_free, u + 1)
                nc.vector.tensor_tensor(comb[:, :, h, :], ts[:, :, 0:DK1], ts[:, :, DK1:PW], ALU.add).then_inc(comb_ready, 1)

            def divide(c):
                dve.wait_ge(comb_ready, H * c + H)
                nc.vector.tensor_scalar(den[:, 0], comb[:, :, :, DK], TINY, None, ALU.max).then_inc(den_ready, 1)
                dve.wait_ge(den_ready, 4 * c + 1)
                nc.vector.reciprocal(den[:, 1], den[:, 0]).then_inc(den_ready, 1)
                dve.wait_ge(den_ready, 4 * c + 2)
                nc.vector.tensor_scalar(den[:, 0], den[:, 1], wtop[:, 2:3], None, ALU.mult).then_inc(den_ready, 1)
                dve.wait_ge(den_ready, 4 * c + 3)
                nc.vector.tensor_tensor(y1[:].rearrange("p s (h d) -> p s h d", h=H), comb[:, :, :, 0:DK],
                                        den[:, 0].unsqueeze(3).to_broadcast([P, SUB, H, DK]), ALU.mult).then_inc(den_ready, 1)
                dve.wait_ge(den_ready, 4 * c + 4)
                dve.wait_ge(out_stored, 16 * c + 16)
                nc.vector.tensor_scalar(y2[:], y1[:], 0.0, None, ALU.min).then_inc(neg_part, 1)

            def finish_sum(c):
                dve.wait_ge(exp_part, c + 1)
                nc.vector.scalar_tensor_tensor(out=y1[:], in0=y1[:], scalar=0.0, in1=y2[:], op0=ALU.max, op1=ALU.add).then_inc(elu_ready, 1)
                dve.wait_ge(elu_ready, c + 1)
                dve.wait_ge(res_loaded, 16 * c + 16)
                nc.vector.scalar_tensor_tensor(out=y1[:], in0=y1[:], scalar=-1.0, in1=xin[:, 0], op0=ALU.add, op1=ALU.add).then_inc(sum_done, 1)
                dve.wait_ge(sum_done, c + 1)
                for s in range(SUB):
                    last = nc.vector.bn_stats(stats[:, s, :], y1[:, s, :])
                last.then_inc(stats_ready, 1)
                dve.wait_ge(stats_ready, 2 * c + 1)
                dve.sem_inc(aggr_begun, 1)
                for s in range(SUB):
                    last = nc.vector.bn_aggr(mv[:, s, :], stats[:, s, :])
                last.then_inc(stats_ready, 1)
                dve.wait_ge(stats_ready, 2 * c + 2)
                nc.vector.tensor_scalar(var[:], mv[:, :, 1], EPS, None, ALU.add).then_inc(var_ready, 1)

            def shifts(c):
                dve.wait_ge(rstd_ready, c + 1)
                nc.vector.scalar_tensor_tensor(out=shift[:], in0=mv[:, :, 0], scalar=-1.0, in1=rstd[:],
                                               op0=ALU.mult, op1=ALU.mult).then_inc(shift_ready, 1)

            aggr_begun = sem("aggr_begun")
            comb_ready, den_ready, elu_ready, stats_ready = sem("comb_ready"), sem("den_ready"), sem("elu_ready"), sem("stats_ready")

            dve.wait_ge(w_loaded, 16)
            dve.wait_ge(a_loaded, 32)
            for i in range(2):
                for kk in range(KT):
                    prod = y1[:, 2 * i + kk, :]
                    last = nc.vector.tensor_tensor(prod, wext[:, kk, 0:D], aw[:, i, :], ALU.mult)
            link(last)
            for i in range(2):
                for kk in range(KT):
                    prod = y1[:, 2 * i + kk, :].rearrange("p (h d) -> p h d", h=H)
                    last = nc.vector.reduce_sum(wext[:, kk, D + i * H:D + (i + 1) * H], prod, AX.X)
            last.then_inc(wext_ready, 1)
            dve.wait_ge(consts_ready, 4)
            for q in range(NB):
                dve.wait_ge(x_turned, q + 1)
                if q >= 2:
                    dve.wait_ge(wh_done, q - 1)
                nc.vector.tensor_copy(xt[:, q % 2, 1, :], tb[:, 1, :]).then_inc(xt_dve, 1)
                cast_adj(0, q) if q < 2 else None
                dve.wait_ge(wh_done, q + 1)
                nc.vector.tensor_copy(slr[:, q], acc[:, :, D:WX]).then_inc(slr_copied, 1)
                dve.wait_ge(wh_copied, q + 1)
                nc.vector.tensor_reduce(out=wmax[:, q:q + 1], in_=wh[:, SUB * q:SUB * (q + 1)].rearrange("p s h d -> p (s h d)"),
                                        op=ALU.max, axis=AX.X)
                nc.vector.tensor_reduce(out=wmax[:, NB + q:NB + q + 1], in_=wh[:, SUB * q:SUB * (q + 1)].rearrange("p s h d -> p (s h d)"),
                                        op=ALU.min, axis=AX.X)
                dve.wait_ge(rows_turned, q + 1)
                if q >= 2:
                    dve.wait_ge(rows_stored[q % 2], 16 * (q // 2))
                link(nc.vector.tensor_copy(rows[:, q % 2, :], rb[0:2 * H, q % 2, :]))
                nc.vector.tensor_reduce(out=rmax[:, q:q + 1], in_=rows[:, q % 2, :], op=ALU.max, axis=AX.X).then_inc(rows_copied, 1)
            dve.wait_ge(rows_copied, NB)
            link(nc.vector.tensor_scalar(wmax[:, NB:2 * NB], wmax[:, NB:2 * NB], -1.0, None, ALU.mult))
            nc.vector.tensor_reduce(out=wmax[:, 2 * NB:2 * NB + 1], in_=wmax[:, 0:2 * NB], op=ALU.max, axis=AX.X).then_inc(wmax_ready, 1)
            link(nc.vector.tensor_reduce(out=rmax[:, NB:NB + 1], in_=rmax[:, 0:NB], op=ALU.max, axis=AX.X))
            nc.vector.tensor_scalar(top[:, 0:2 * H], ident[0:2 * H, 0:2 * H], rmax[:, NB:NB + 1], None, ALU.mult)
            dve.wait_ge(wmax_turned, 1)
            nc.vector.tensor_reduce(out=top[0:1, 2 * H:2 * H + 1], in_=rb[0:1, 1, 0:P], op=ALU.max, axis=AX.X).then_inc(top_ready, 1)
            dve.wait_ge(smax_done, 1)
            nc.vector.tensor_copy(wtop[:, 0:1], rb[:, 0, 2 * H:2 * H + 1])
            link(nc.vector.tensor_copy(smax[:], rb[:, 0, 0:2 * H]))
            flat = lambda t: t.rearrange("p q s h -> p (q s) h")
            smax_all = smax[:, H:2 * H].unsqueeze(1).to_broadcast([P, NB * SUB, H])
            nc.vector.tensor_tensor(flat(t32[:]), flat(slr[:, :, :, H:2 * H]), smax_all, ALU.subtract).then_inc(args_ready, 1)
            link(nc.vector.tensor_tensor(flat(cn[:]), flat(slr[:, :, :, 0:H]), smax_all, ALU.add))
            nc.vector.tensor_scalar(cn[:], cn[:], 0.0, None, ALU.max).then_inc(args_ready, 1)
            nc.vector.tensor_scalar(nsr[:], slr[:, :, :, H:2 * H], -1.0, None, ALU.mult)
            link(nc.vector.reciprocal(wtop[:, 1:2], wtop[:, 0:1]))
            nc.vector.tensor_scalar(wtop[:, 2:3], wtop[:, 0:1], WIDE1 / WIDE, None, ALU.mult)
            link(nc.vector.tensor_scalar(wtop[:, 1:2], wtop[:, 1:2], WIDE, None, ALU.mult))
            for q in range(NB):
                nc.vector.tensor_scalar(wh[:, SUB * q:SUB * (q + 1), :, 0:DK], wh[:, SUB * q:SUB * (q + 1), :, 0:DK], wtop[:, 1:2], None, ALU.mult)
            link(nc.vector.tensor_scalar(wh[:, :, :, DK], wh[:, :, :, DK], WIDE1, None, ALU.mult))
            dve.wait_ge(exps_ready, 1)
            for q in range(NB):
                for i, f in enumerate((full, full2)):
                    if q >= 1:
                        dve.wait_ge(parts_ready, q)
                    nc.vector.tensor_tensor(f[:], wh[:, SUB * q:SUB * (q + 1)],
                                            bd[:, i, q].unsqueeze(3).to_broadcast([P, SUB, H, DK1]), ALU.mult).then_inc(full_ready, 1)
                for i, f in enumerate((full, full2)):
                    dve.wait_ge(head_ready, 2 * q + i + 1)
                    last = nc.vector.tensor_tensor(parts[:, q, :, :, i, DK1:PW], f[:], parts[:, q, :, :, i, 0:DK1], ALU.subtract)
                last.then_inc(parts_ready, 1)
            for q in range(NB):
                if q >= 2:
                    cast_adj(0, q)
                if q >= 1:
                    take_mask(0, q - 1)
            take_mask(0, NB - 1)

            def unit(c, h, prep, epilogue):
                for k in range(NQ):
                    compare(c, h, k)
                    t = NQ * (h - 1) + k
                    if prep and h > 0:
                        if t - 1 in CASTS:
                            take_mask(c + 1, CASTS[t - 1])
                        if t in CASTS:
                            cast_adj(c + 1, CASTS[t])
                    pair(c, h, k)
                    if k == 0 and h > 0:
                        add_sums(c, h - 1)
                    if epilogue:
                        if k == 0:
                            take_mask(c, NB - 1)
                            add_sums(c - 1, H - 1)
                        if k == 1:
                            divide(c - 1)
                        if k == 3:
                            finish_sum(c - 1)
                if epilogue:
                    shifts(c - 1)

            unit(0, 0, False, False)
            with dve.Fori(0, NB - 1) as c:
                for h in range(1, H):
                    unit(c, h, True, False)
                unit(c + 1, 0, False, True)
            for h in range(1, H):
                unit(NB - 1, h, False, False)
            add_sums(NB - 1, H - 1)
            divide(NB - 1)
            finish_sum(NB - 1)
            shifts(NB - 1)


_INS = ["x", "adj", "L0_gnn_W", "L0_gnn_a_l", "L0_gnn_a_r"]


def kernel(**inputs):
    import numpy as np
    import concourse.bacc as bacc
    from concourse import mybir
    from concourse.bass_utils import run_bass_kernel_spmd

    nc = bacc.Bacc("TRN2", target_bir_lowering=False, num_devices=1, dynamic_dma_scratch_size=1024)
    arrays, args = {}, []
    for name in _INS:
        a = np.ascontiguousarray(inputs[name])
        arrays[f"in_{name}"] = a
        args.append(nc.dram_tensor(f"in_{name}", a.shape, mybir.dt.from_np(a.dtype), kind="ExternalInput").ap())
    n, d = inputs["x"].shape
    heads = inputs["L0_gnn_a_l"].shape[0]
    sl_rows = nc.dram_tensor("sl_rows", (heads, n), mybir.dt.float32, kind="Internal").ap()
    out = nc.dram_tensor("out", (n, d), mybir.dt.float32, kind="ExternalOutput").ap()
    graph_attention(nc, *args, sl_rows, out)
    r = run_bass_kernel_spmd(nc, [arrays], core_ids=[0])
    return r.results[0]["out"]
```

```python
def graph_attention(nc, x, adj, w, a_l, a_r, sl_rows, out):
    from contextlib import ExitStack
    from concourse import mybir

    dt, ALU, ACT = mybir.dt, mybir.AluOpType, mybir.ActivationFunctionType
    AX = mybir.AxisListType
    F32, F16, I32, U32, U8, I8, F8 = dt.float32, dt.float16, dt.int32, dt.uint32, dt.uint8, dt.int8, dt.float8e4

    P = 128
    N, D = x.shape
    H, DK = a_l.shape
    SUB = 4
    BLK = SUB * P
    NB = N // BLK
    KT = D // P
    DK1 = DK + 1
    PW = 2 * DK1
    WX = D + 2 * H
    QB = 2
    NQ = NB // QB
    WORDS = QB * BLK
    SHARE = (6, 6, 6, 6)
    K_SCALE, K_ADD = 1, 1
    BIT = 0x20
    EDGE, CODE0 = 0x01010101, 0x40
    WIDE = 2.0 ** 13
    WIDE1 = 2.0 ** 14
    TINY = 1e-30
    EPS = 1e-5

    ctx = ExitStack()
    with ctx:
        def sb(name, shape, t):
            return ctx.enter_context(nc.sbuf_tensor(name, shape, t))

        def pb(name, shape, t):
            return ctx.enter_context(nc.psum_tensor(name, shape, t))

        def sem(name):
            return ctx.enter_context(nc.semaphore(name))

        ident = sb("ident", [P, P], F32)
        eye = sb("eye", [P, SUB, BLK], I32)
        ones = sb("ones", [2 * H, P], F32)
        half = sb("half", [P, SUB], F32)
        wext = sb("wext", [P, KT, WX], F32)
        slr = sb("slr", [P, NB, SUB, 2 * H], F32)
        nsr = sb("nsr", [P, NB, SUB, H], F32)
        bd = sb("bd", [P, 2, NB, SUB, H], F32)
        cn = sb("cn", [P, NB, SUB, H], F32)
        rmax = sb("rmax", [2 * H, NB + 1], F32)
        wmax = sb("wmax", [P, NB + 1], F32)
        top = sb("top", [2 * H, 2 * H + 1], F32)
        smax = sb("smax", [P, 2 * H], F32)
        wtop = sb("wtop", [P, 4], F32)
        parts = sb("parts", [P, NB, SUB, H, 2, PW], F16)
        room = sb("room", [P, NB * SUB * H * DK1], F32)
        wh = room[:, :].rearrange("p (m h d) -> p m h d", h=H, d=DK1)
        o_slb, o_sgn, o_pair = 0, H * BLK, H * BLK + 2 * WORDS
        slb = room[:, o_slb:o_sgn].rearrange("p (h n) -> p h n", h=H)
        sgn = room[:, o_sgn:o_pair].bitcast(U32).rearrange("p (s w) -> p s w", s=2)
        room2 = sb("room2", [P, 4 * WORDS], F32)
        o_rows = 2 * KT * BLK
        xt = room2[:, 0:o_rows].rearrange("p (s k n) -> p s k n", s=2, k=KT)
        rows = room2[0:2 * H, o_rows:o_rows + 2 * BLK].rearrange("p (s n) -> p s n", s=2)
        aw = room2[:, o_rows + 2 * BLK:o_rows + 2 * BLK + 2 * D].rearrange("p (i d) -> p i d", i=2)
        halves = (room[:, o_pair:o_pair + 4 * WORDS].bitcast(U32), room2[:].bitcast(U32))
        pairs = [tuple(halves[k // 2][:, (2 * (k % 2) + i) * WORDS:(2 * (k % 2) + i + 1) * WORDS] for i in range(2))
                 for k in range(NQ)]
        adj_in = sb("adj_in", [P, 2, SUB, BLK], I32)
        adj_by = sb("adj_by", [P, 2, SUB * BLK], U8)
        mask = sb("mask", [P, 2, NB, BLK], U32)
        xin = sb("xin", [P, 2, SUB, D], F32)
        comb = sb("comb", [P, SUB, H, DK1], F32)
        td = sb("td", [P, SUB, PW], F32)
        ts = sb("ts", [P, SUB, PW], F32)
        den = sb("den", [P, 2, SUB, H], F32)
        y1 = sb("y1", [P, SUB, D], F32)
        y2 = sb("y2", [P, SUB, D], F32)
        stats = sb("stats", [P, SUB, 6], F32)
        mv = sb("mv", [P, SUB, 2], F32)
        var = sb("var", [P, SUB], F32)
        rstd = sb("rstd", [P, SUB], F32)
        shift = sb("shift", [P, SUB], F32)
        full = sb("full", [P, SUB, H, DK1], F32)
        full2 = sb("full2", [P, SUB, H, DK1], F32)
        t32 = sb("t32", [P, NB, SUB, H], F32)

        acc = pb("acc", [P, SUB, 512], F32)
        tb = pb("tb", [P, 2, 512], F32)
        rb = pb("rb", [P, 2, 512], F32)

        w_loaded, a_loaded = sem("w_loaded"), sem("a_loaded")
        x_loaded = [sem(f"x_loaded{i}") for i in range(2)]
        adj_loaded = [sem(f"adj_loaded{i}") for i in range(2)]
        rows_stored = [sem(f"rows_stored{i}") for i in range(2)]
        sl_loaded = [sem(f"sl_loaded{h}") for h in range(H)]
        res_loaded, out_stored = sem("res_loaded"), sem("out_stored")
        consts_ready, wext_ready = sem("consts_ready"), sem("wext_ready")
        x_turned, xt_act, xt_dve = sem("x_turned"), sem("xt_act"), sem("xt_dve")
        wh_done, wh_copied, slr_copied = sem("wh_done"), sem("wh_copied"), sem("slr_copied")
        rows_turned, rows_copied, top_ready = sem("rows_turned"), sem("rows_copied"), sem("top_ready")
        wmax_ready, wmax_turned, smax_done, exps_ready = sem("wmax_ready"), sem("wmax_turned"), sem("smax_done"), sem("exps_ready")
        args_ready, cn_ready = sem("args_ready"), sem("cn_ready")
        full_ready, head_ready, parts_ready = sem("full_ready"), sem("head_ready"), sem("parts_ready")
        diag_fixed, bytes_ready, mask_turned, mask_ready = sem("diag_fixed"), sem("bytes_ready"), sem("mask_turned"), sem("mask_ready")
        cmp_act, cmp_dve, pair_ready, quarter_done = sem("cmp_act"), sem("cmp_dve"), sem("pair_ready"), sem("quarter_done")
        quarter_begun = sem("quarter_begun")
        acc_done, d_scaled, acc_free = sem("acc_done"), sem("d_scaled"), sem("acc_free")
        neg_part, exp_part, sum_done, var_ready = sem("neg_part"), sem("exp_part"), sem("sum_done"), sem("var_ready")
        rstd_ready, shift_ready, norm_done = sem("rstd_ready"), sem("shift_ready"), sem("norm_done")
        dve_order, act_order, pool_order = sem("dve_order"), sem("act_order"), sem("pool_order")

        assert NB == H // 2 * NQ

        def count_diag(c, q):
            return (c * (NB - 1) + (q + NB)) >> 3

        block = ctx.enter_context(nc.Block())

        @block.sync
        def _(sp):
            def load_adj(c, q):
                if isinstance(c, int) and c == 0:
                    src = adj[0:BLK, q * BLK:(q + 1) * BLK]
                else:
                    src = adj.rearrange("(c r) m -> c r m", r=BLK)[c, :, q * BLK:(q + 1) * BLK]
                if not isinstance(c, int) or NB * c + q >= 2:
                    sp.wait_ge(bytes_ready, NB * c + (q - 1))
                sp.dma_start(adj_in[:, q % 2], src.rearrange("(p s) m -> p s m", s=SUB)).then_inc(adj_loaded[q % 2], 16)

            def load_sl(c, h):
                if not isinstance(c, int):
                    sp.wait_ge(cmp_act, 4 * H * (c - 1) + (4 * h + 4))
                    sp.wait_ge(cmp_dve, 4 * H * (c - 1) + (4 * h + 4))
                src = sl_rows.rearrange("h (c n) -> c h n", n=BLK)[c, h:h + 1, :]
                sp.dma_start(slb[:, h, :], src.to_broadcast([P, BLK])).then_inc(sl_loaded[h], 16)

            def load_res(c):
                src = x.rearrange("(c p s) d -> c p s d", p=P, s=SUB)[c]
                sp.dma_start(xin[:, 0], src).then_inc(res_loaded, 16)

            sp.dma_start(wext[:, :, 0:D], w.rearrange("(k p) d -> p k d", p=P)).then_inc(w_loaded, 16)
            for i, a in enumerate((a_l, a_r)):
                sp.dma_start(aw[:, i, :], a.rearrange("h d -> (h d)").unsqueeze(0).to_broadcast([P, D])).then_inc(a_loaded, 16)
            def load_x(q):
                if q >= 2:
                    sp.wait_ge(x_turned, q - 1)
                sp.dma_start(xin[:, q % 2], x[q * BLK:(q + 1) * BLK, :].rearrange("(p s) d -> p s d", s=SUB)).then_inc(x_loaded[q % 2], 16)

            load_x(0)
            load_adj(0, 0)
            load_x(1)
            load_adj(0, 1)
            for q in range(NB):
                if q + 2 < NB:
                    load_adj(0, q + 2)
                    load_x(q + 2)
                sp.wait_ge(rows_copied, q + 1)
                sp.dma_start(sl_rows[:, q * BLK:(q + 1) * BLK], rows[0:H, q % 2, :]).then_inc(rows_stored[q % 2], 16)
            for i in range(2):
                sp.wait_ge(rows_stored[i], 16 * (NB // 2))
            sp.wait_ge(parts_ready, NB)
            for h in range(H):
                load_sl(0, h)
            load_res(0)
            with sp.Fori(0, NB - 1) as c:
                load_adj(c + 1, 0)
                load_adj(c + 1, 1)
                load_sl(c + 1, 0)
                load_sl(c + 1, 1)
                for q in range(2, 6):
                    load_adj(c + 1, q)
                load_sl(c + 1, 2)
                load_adj(c + 1, 6)
                load_adj(c + 1, 7)
                load_sl(c + 1, 3)
                sp.wait_ge(sum_done, c + 1)
                load_res(c + 1)

        @block.gpsimd
        def _(pool):
            links = [0]

            def link(ins):
                links[0] += 1
                ins.then_inc(pool_order, 1)
                pool.wait_ge(pool_order, links[0])

            link(nc.gpsimd.memset(ident[:], 0.0))
            nc.gpsimd.affine_select(out=ident[:], in_=ident[:], compare_op=ALU.not_equal, fill=1.0, base=0,
                                    pattern=[[-1, P]], channel_multiplier=1).then_inc(consts_ready, 1)
            nc.gpsimd.memset(ones[:], 1.0).then_inc(consts_ready, 1)
            nc.gpsimd.memset(wh[:, :, :, DK:DK1], 1.0).then_inc(consts_ready, 1)
            nc.gpsimd.memset(half[:], -0.5).then_inc(consts_ready, 1)
            pool.sem_inc(out_stored, 16)
            link(nc.gpsimd.memset(eye[:], 0))
            link(nc.gpsimd.affine_select(out=eye[:], in_=eye[:], compare_op=ALU.not_equal, fill=1.0, base=0,
                                         pattern=[[1, SUB], [-1, BLK]], channel_multiplier=SUB))

            def fix_diag(c):
                pool.wait_ge(adj_loaded[0], 16 * (4 * c + ((c >> 1) + 1)))
                if not isinstance(c, int):
                    pool.wait_ge(adj_loaded[1], 16 * (4 * c + ((c + 1) >> 1)))
                slot = adj_in[:, c & 1]
                nc.gpsimd.tensor_tensor(slot, slot, eye[:], ALU.add).then_inc(diag_fixed, 1)

            def inverse_root(c):
                pool.wait_ge(var_ready, c + 1)
                nc.gpsimd.tensor_tensor(rstd[:], var[:], half[:], ALU.pow).then_inc(rstd_ready, 1)

            fix_diag(0)
            with pool.Fori(0, NB - 1) as c:
                fix_diag(c + 1)
                inverse_root(c)
            inverse_root(NB - 1)

        @block.tensor
        def _(pe):
            def turn_mask(c, q):
                pe.wait_ge(bytes_ready, NB * c + (q + 1))
                start = isinstance(c, int)
                if not start:
                    pe.wait_ge(mask_ready, NB * c + (q - 1))
                elif q >= 1:
                    pe.wait_ge(mask_ready, q)
                bank = rb[:, 1, :] if start else tb[:, q % 2, :]
                by = adj_by[:, q % 2, :].bitcast(F32).rearrange("p (s w) -> p s w", s=SUB)
                for s in range(SUB):
                    last = nc.tensor.transpose(bank[:, s * P:(s + 1) * P], by[:, s, :], ident[:])
                last.then_inc(mask_turned, 1)

            def unit(c, h, prep):
                u = H * c + h
                for k in range(NQ):
                    if prep:
                        turn_mask(c + 1, NQ * (h - H // 2) + k)
                    pe.wait_ge(pair_ready, NQ * u + (k + 1))
                    by = [m.bitcast(F8).rearrange("p (q s j b) -> p q s j b", q=QB, s=SUB, b=SUB)
                          for m in pairs[k]]
                    if k == 0 and (not isinstance(c, int) or u >= 1):
                        pe.wait_ge(acc_free, u)
                    pe.sem_inc(quarter_begun, 1)
                    for s in range(SUB):
                        for q in range(QB):
                            for b in range(SUB):
                                for i in range(2):
                                    first = k == 0 and q == 0 and b == 0
                                    final = k == NQ - 1 and q == QB - 1 and b == SUB - 1
                                    last = nc.tensor.matmul(acc[:, s, i * PW:(i + 1) * PW], by[i][:, q, s, :, b],
                                                            parts[:, QB * k + q, b, h, i, :],
                                                            start=first and i == 0, stop=final, skip_group_check=True)
                        if k == NQ - 1 and s < SUB - 1:
                            last.then_inc(acc_done, 1)
                    last.then_inc(quarter_done, 1)

            def turn_x(q):
                pe.wait_ge(x_loaded[q % 2], 16 * (q // 2 + 1))
                if q >= 1:
                    pe.wait_ge(xt_act, q)
                    pe.wait_ge(xt_dve, q)
                for kk in range(KT):
                    for s in range(SUB):
                        last = nc.tensor.transpose(tb[:, kk, s * P:(s + 1) * P], xin[:, q % 2, s, kk * P:(kk + 1) * P], ident[:])
                last.then_inc(x_turned, 1)

            def turn_rows(q):
                pe.wait_ge(slr_copied, q + 1)
                if q >= 1:
                    pe.wait_ge(rows_copied, q)
                for s in range(SUB):
                    last = nc.tensor.transpose(rb[0:2 * H, 0, s * P:(s + 1) * P], slr[:, q, s, :], ident[:])
                last.then_inc(rows_turned, 1)

            pe.wait_ge(consts_ready, 4)
            turn_x(0)
            for q in range(NB):
                turn_mask(0, q)
                pe.wait_ge(xt_act, q + 1)
                pe.wait_ge(xt_dve, q + 1)
                if q == 0:
                    pe.wait_ge(wext_ready, 1)
                else:
                    pe.wait_ge(wh_copied, q)
                for s in range(SUB):
                    for kk in range(KT):
                        last = nc.tensor.matmul(acc[:, s, 0:WX], xt[:, q % 2, kk, s * P:(s + 1) * P], wext[:, kk, :],
                                                start=kk == 0, stop=kk == KT - 1)
                last.then_inc(wh_done, 1)
                if q + 1 < NB:
                    turn_x(q + 1)
                turn_rows(q)
            pe.wait_ge(wmax_ready, 1)
            pe.wait_ge(rows_copied, NB)
            pe.wait_ge(mask_ready, NB)
            nc.tensor.transpose(rb[0:1, 1, 0:P], wmax[:, NB:NB + 1], ident[:]).then_inc(wmax_turned, 1)
            pe.wait_ge(top_ready, 1)
            nc.tensor.matmul(rb[:, 0, 0:2 * H], ones[:, :], top[:, 0:2 * H], start=True, stop=True)
            nc.tensor.matmul(rb[:, 0, 2 * H:2 * H + 1], ones[0:1, :], top[0:1, 2 * H:2 * H + 1], start=False, stop=True,
                             skip_group_check=True).then_inc(smax_done, 1)
            pe.wait_ge(parts_ready, NB)
            for h in range(0, H // 2):
                unit(0, h, False)
            with pe.Fori(0, NB - 1) as c:
                for h in range(H // 2, H):
                    unit(c, h, True)
                for h in range(0, H // 2):
                    unit(c + 1, h, False)
            for h in range(H // 2, H):
                unit(NB - 1, h, False)

        @block.scalar
        def _(act):
            def compare(c, h, k, between=None):
                g = NQ * (H * c + h) + k
                if k == 0:
                    act.wait_ge(sl_loaded[h], 16 * c + 16)
                if not isinstance(c, int) or g >= 2:
                    act.wait_ge(pair_ready, g - 1)
                to = sgn[:, k % 2, :].bitcast(I8).rearrange("p (q n b) -> p q n b", q=QB, b=SUB)
                for i in range(SHARE[h]):
                    q, b = i // SUB, i % SUB
                    last = nc.scalar.activation(to[:, q, :, b], slb[:, h, :], ACT.Sign,
                                                bias=slr[:, QB * k + q, b, H + h:H + h + 1])
                    if i == SHARE[h] - 1:
                        last.then_inc(cmp_act, 1)
                    if between is not None and i >= SHARE[h] - SUB:
                        scale_d(*between, i - (SHARE[h] - SUB))

            def scale_d(c, h, s):
                u = H * c + h
                if s == 0 and (not isinstance(c, int) or u >= 1):
                    act.wait_ge(acc_free, u)
                if s < SUB - 1:
                    act.wait_ge(acc_done, (SUB - 1) * u + (s + 1))
                else:
                    act.wait_ge(quarter_done, NQ * u + NQ)
                ins = nc.scalar.activation(td[:, s, :], acc[:, s, PW:2 * PW], ACT.Copy, scale=cn[:, c, s, h:h + 1])
                if s == SUB - 1:
                    ins.then_inc(d_scaled, 1)

            def exp_negative(c):
                act.wait_ge(neg_part, c + 1)
                nc.scalar.activation(y2[:], y2[:], ACT.Exp).then_inc(exp_part, 1)

            def normalize(c):
                act.wait_ge(shift_ready, c + 1)
                for s in range(SUB):
                    last = nc.scalar.activation(y2[:, s, :], y1[:, s, :], ACT.Identity, bias=shift[:, s:s + 1],
                                                scale=rstd[:, s:s + 1])
                last.then_inc(norm_done, 1)

            def store(c):
                act.wait_ge(norm_done, c + 1)
                act.dma_start(out.rearrange("(c p s) d -> c p s d", p=P, s=SUB)[c], y2[:]).then_inc(out_stored, 16)

            def take_x(q):
                act.wait_ge(x_turned, q + 1)
                if q >= 2:
                    act.wait_ge(wh_done, q - 1)
                nc.scalar.copy(xt[:, q % 2, 0, :], tb[:, 0, :]).then_inc(xt_act, 1)

            take_x(0)
            for q in range(NB):
                act.wait_ge(slr_copied, q + 1)
                nc.scalar.copy(wh[:, SUB * q:SUB * (q + 1), :, 0:DK],
                               acc[:, :, 0:D].rearrange("p s (h d) -> p s h d", h=H)).then_inc(wh_copied, 1)
                if q + 1 < NB:
                    take_x(q + 1)
            act.wait_ge(args_ready, 1)
            nc.scalar.activation(bd[:, 0], t32[:], ACT.Exp)
            nc.scalar.activation(bd[:, 1], t32[:], ACT.Exp, scale=0.2).then_inc(exps_ready, 1)
            act.wait_ge(args_ready, 2)
            nc.scalar.activation(cn[:], cn[:], ACT.Exp, scale=-0.8).then_inc(cn_ready, 1)
            for q in range(NB):
                for i, f in enumerate((full, full2)):
                    act.wait_ge(full_ready, 2 * q + i + 1)
                    nc.scalar.copy(parts[:, q, :, :, i, 0:DK1], f[:]).then_inc(head_ready, 1)

            def unit(c, h, last_unit, epilogue=False):
                for k in range(NQ):
                    compare(c, h, k, last_unit if k == K_SCALE else None)
                    if epilogue and h == 0 and k == 2:
                        exp_negative(c - 1)
                    if epilogue and h == 1 and k == 1:
                        normalize(c - 1)
                    if epilogue and h == 1 and k == 2:
                        store(c - 1)

            act.wait_ge(cn_ready, 1)
            unit(0, 0, None)
            unit(0, 1, (0, 0))
            with act.Fori(0, NB - 1) as c:
                for h in range(H // 2, H):
                    unit(c, h, (c, h - 1))
                unit(c + 1, 0, (c, H - 1), True)
                unit(c + 1, 1, (c + 1, 0), True)
            for h in range(H // 2, H):
                unit(NB - 1, h, (NB - 1, h - 1))
            for s in range(SUB):
                scale_d(NB - 1, H - 1, s)
            exp_negative(NB - 1)
            normalize(NB - 1)
            store(NB - 1)
            act.wait_ge(out_stored, 16 * NB + 16)

        @block.vector
        def _(dve):
            links = [0]

            def link(ins):
                links[0] += 1
                ins.then_inc(dve_order, 1)
                dve.wait_ge(dve_order, links[0])

            def cast_adj(c, q):
                dve.wait_ge(adj_loaded[q % 2], 16 * (4 * c + (q // 2 + 1)))
                dve.wait_ge(diag_fixed, count_diag(c, q))
                if not isinstance(c, int) or NB * c + q >= 2:
                    dve.wait_ge(mask_turned, NB * c + (q - 1))
                nc.vector.tensor_scalar(adj_by[:, q % 2, :], adj_in[:, q % 2].rearrange("p s m -> p (s m)"), 0.0, float(CODE0),
                                        ALU.is_gt, ALU.add).then_inc(bytes_ready, 1)

            def take_mask(c, q):
                dve.wait_ge(mask_turned, NB * c + (q + 1))
                bank = rb[:, 1, :] if isinstance(c, int) else tb[:, q % 2, :]
                nc.vector.tensor_scalar(mask[:, c & 1, q, :], bank.bitcast(U32), EDGE, 5,
                                        ALU.bitwise_and, ALU.logical_shift_left).then_inc(mask_ready, 1)

            def compare(c, h, k):
                if k == 0:
                    dve.wait_ge(sl_loaded[h], 16 * c + 16)
                to = sgn[:, k % 2, :].bitcast(U8).rearrange("p (q n b) -> p q n b", q=QB, b=SUB)
                for i in range(SHARE[h], QB * SUB):
                    q, b = i // SUB, i % SUB
                    last = nc.vector.tensor_scalar(to[:, q, :, b], slb[:, h, :], nsr[:, QB * k + q, b, h:h + 1],
                                                   float(BIT), ALU.is_le, ALU.mult)
                last.then_inc(cmp_dve, 1)

            def pair(c, h, k):
                g = NQ * (H * c + h) + k
                dve.wait_ge(cmp_act, g + 1)
                dve.wait_ge(cmp_dve, g + 1)
                dve.wait_ge(mask_ready, NB * c + QB * (k + 1))
                if not isinstance(c, int) or g >= NQ:
                    dve.wait_ge(quarter_done, g - (NQ - 1))
                m = mask[:, c & 1, QB * k:QB * (k + 1), :].rearrange("p q n -> p (q n)")
                nc.vector.tensor_tensor(pairs[k][1], sgn[:, k % 2, :], m, ALU.bitwise_and)
                nc.vector.scalar_tensor_tensor(out=pairs[k][0], in0=sgn[:, k % 2, :], scalar=BIT * EDGE, in1=m,
                                               op0=ALU.bitwise_xor, op1=ALU.bitwise_and).then_inc(pair_ready, 1)

            def add_sums(c, h):
                u = H * c + h
                dve.wait_ge(d_scaled, u + 1)
                nc.vector.tensor_tensor(ts[:], acc[:, :, 0:PW], td[:], ALU.add).then_inc(acc_free, 1)
                dve.wait_ge(acc_free, u + 1)
                nc.vector.tensor_tensor(comb[:, :, h, :], ts[:, :, 0:DK1], ts[:, :, DK1:PW], ALU.add).then_inc(comb_ready, 1)

            def divide(c):
                dve.wait_ge(comb_ready, H * c + H)
                nc.vector.tensor_scalar(den[:, 0], comb[:, :, :, DK], TINY, None, ALU.max).then_inc(den_ready, 1)
                dve.wait_ge(den_ready, 4 * c + 1)
                nc.vector.reciprocal(den[:, 1], den[:, 0]).then_inc(den_ready, 1)
                dve.wait_ge(den_ready, 4 * c + 2)
                nc.vector.tensor_scalar(den[:, 0], den[:, 1], wtop[:, 2:3], None, ALU.mult).then_inc(den_ready, 1)
                dve.wait_ge(den_ready, 4 * c + 3)
                nc.vector.tensor_tensor(y1[:].rearrange("p s (h d) -> p s h d", h=H), comb[:, :, :, 0:DK],
                                        den[:, 0].unsqueeze(3).to_broadcast([P, SUB, H, DK]), ALU.mult).then_inc(den_ready, 1)
                dve.wait_ge(den_ready, 4 * c + 4)
                dve.wait_ge(out_stored, 16 * c + 16)
                nc.vector.tensor_scalar(y2[:], y1[:], 0.0, None, ALU.min).then_inc(neg_part, 1)

            def finish_sum(c):
                dve.wait_ge(exp_part, c + 1)
                nc.vector.scalar_tensor_tensor(out=y1[:], in0=y1[:], scalar=0.0, in1=y2[:], op0=ALU.max, op1=ALU.add).then_inc(elu_ready, 1)
                dve.wait_ge(elu_ready, c + 1)
                dve.wait_ge(res_loaded, 16 * c + 16)
                nc.vector.scalar_tensor_tensor(out=y1[:], in0=y1[:], scalar=-1.0, in1=xin[:, 0], op0=ALU.add, op1=ALU.add).then_inc(sum_done, 1)
                dve.wait_ge(sum_done, c + 1)
                for s in range(SUB):
                    last = nc.vector.bn_stats(stats[:, s, :], y1[:, s, :])
                last.then_inc(stats_ready, 1)
                dve.wait_ge(stats_ready, 2 * c + 1)
                dve.sem_inc(aggr_begun, 1)
                for s in range(SUB):
                    last = nc.vector.bn_aggr(mv[:, s, :], stats[:, s, :])
                last.then_inc(stats_ready, 1)
                dve.wait_ge(stats_ready, 2 * c + 2)
                nc.vector.tensor_scalar(var[:], mv[:, :, 1], EPS, None, ALU.add).then_inc(var_ready, 1)

            def shifts(c):
                dve.wait_ge(rstd_ready, c + 1)
                nc.vector.scalar_tensor_tensor(out=shift[:], in0=mv[:, :, 0], scalar=-1.0, in1=rstd[:],
                                               op0=ALU.mult, op1=ALU.mult).then_inc(shift_ready, 1)

            rmax_ready, aggr_begun = sem("rmax_ready"), sem("aggr_begun")
            comb_ready, den_ready, elu_ready, stats_ready = sem("comb_ready"), sem("den_ready"), sem("elu_ready"), sem("stats_ready")

            dve.wait_ge(w_loaded, 16)
            dve.wait_ge(a_loaded, 32)
            for i in range(2):
                for kk in range(KT):
                    prod = y1[:, 2 * i + kk, :]
                    last = nc.vector.tensor_tensor(prod, wext[:, kk, 0:D], aw[:, i, :], ALU.mult)
            link(last)
            for i in range(2):
                for kk in range(KT):
                    prod = y1[:, 2 * i + kk, :].rearrange("p (h d) -> p h d", h=H)
                    last = nc.vector.reduce_sum(wext[:, kk, D + i * H:D + (i + 1) * H], prod, AX.X)
            last.then_inc(wext_ready, 1)
            dve.wait_ge(consts_ready, 4)

            def take_x(q):
                dve.wait_ge(x_turned, q + 1)
                if q >= 2:
                    dve.wait_ge(wh_done, q - 1)
                nc.vector.tensor_copy(xt[:, q % 2, 1, :], tb[:, 1, :]).then_inc(xt_dve, 1)

            cast_adj(0, 0)
            take_x(0)
            for q in range(NB):
                if q + 1 < NB:
                    cast_adj(0, q + 1)
                take_mask(0, q)
                dve.wait_ge(wh_done, q + 1)
                nc.vector.tensor_copy(slr[:, q], acc[:, :, D:WX]).then_inc(slr_copied, 1)
                if q + 1 < NB:
                    take_x(q + 1)
                dve.wait_ge(rows_turned, q + 1)
                if q >= 2:
                    dve.wait_ge(rows_stored[q % 2], 16 * (q // 2))
                nc.vector.tensor_copy(rows[:, q % 2, :], rb[0:2 * H, 0, :]).then_inc(rows_copied, 1)
                dve.wait_ge(wh_copied, q + 1)
                nc.vector.tensor_reduce(out=wmax[:, q:q + 1], in_=wh[:, SUB * q:SUB * (q + 1)].rearrange("p s h d -> p (s h d)"),
                                        op=ALU.max, axis=AX.X, apply_absolute_value=True)
                dve.wait_ge(rows_copied, q + 1)
                nc.vector.tensor_reduce(out=rmax[:, q:q + 1], in_=rows[:, q % 2, :], op=ALU.max, axis=AX.X).then_inc(rmax_ready, 1)
            dve.wait_ge(rmax_ready, NB)
            nc.vector.tensor_reduce(out=wmax[:, NB:NB + 1], in_=wmax[:, 0:NB], op=ALU.max, axis=AX.X).then_inc(wmax_ready, 1)
            link(nc.vector.tensor_reduce(out=rmax[:, NB:NB + 1], in_=rmax[:, 0:NB], op=ALU.max, axis=AX.X))
            nc.vector.tensor_scalar(top[:, 0:2 * H], ident[0:2 * H, 0:2 * H], rmax[:, NB:NB + 1], None, ALU.mult)
            dve.wait_ge(wmax_turned, 1)
            nc.vector.tensor_reduce(out=top[0:1, 2 * H:2 * H + 1], in_=rb[0:1, 1, 0:P], op=ALU.max, axis=AX.X).then_inc(top_ready, 1)
            dve.wait_ge(smax_done, 1)
            nc.vector.tensor_copy(wtop[:, 0:1], rb[:, 0, 2 * H:2 * H + 1])
            link(nc.vector.tensor_copy(smax[:], rb[:, 0, 0:2 * H]))
            flat = lambda t: t.rearrange("p q s h -> p (q s) h")
            smax_all = smax[:, H:2 * H].unsqueeze(1).to_broadcast([P, NB * SUB, H])
            nc.vector.tensor_tensor(flat(t32[:]), flat(slr[:, :, :, H:2 * H]), smax_all, ALU.subtract).then_inc(args_ready, 1)
            link(nc.vector.tensor_tensor(flat(cn[:]), flat(slr[:, :, :, 0:H]), smax_all, ALU.add))
            nc.vector.tensor_scalar(cn[:], cn[:], 0.0, None, ALU.max).then_inc(args_ready, 1)
            nc.vector.tensor_scalar(nsr[:], slr[:, :, :, H:2 * H], -1.0, None, ALU.mult)
            link(nc.vector.reciprocal(wtop[:, 1:2], wtop[:, 0:1]))
            nc.vector.tensor_scalar(wtop[:, 2:3], wtop[:, 0:1], WIDE1 / WIDE, None, ALU.mult)
            link(nc.vector.tensor_scalar(wtop[:, 1:2], wtop[:, 1:2], WIDE, None, ALU.mult))
            link(nc.vector.reciprocal(wtop[:, 3:4], wtop[:, 1:2]))
            link(nc.vector.tensor_scalar(wtop[:, 3:4], wtop[:, 3:4], WIDE1, None, ALU.mult))
            link(nc.vector.tensor_scalar(wh[:, :, :, DK], wh[:, :, :, DK], wtop[:, 3:4], None, ALU.mult))
            dve.wait_ge(exps_ready, 1)
            link(nc.vector.tensor_scalar(bd[:], bd[:], wtop[:, 1:2], None, ALU.mult))
            for q in range(NB):
                for i, f in enumerate((full, full2)):
                    if q >= 1:
                        dve.wait_ge(parts_ready, q)
                    nc.vector.tensor_tensor(f[:], wh[:, SUB * q:SUB * (q + 1)],
                                            bd[:, i, q].unsqueeze(3).to_broadcast([P, SUB, H, DK1]), ALU.mult).then_inc(full_ready, 1)
                for i, f in enumerate((full, full2)):
                    dve.wait_ge(head_ready, 2 * q + i + 1)
                    last = nc.vector.tensor_tensor(parts[:, q, :, :, i, DK1:PW], f[:], parts[:, q, :, :, i, 0:DK1], ALU.subtract)
                last.then_inc(parts_ready, 1)

            def unit(c, h, prep, epilogue, last_unit):
                for k in range(NQ):
                    compare(c, h, k)
                    if k == K_ADD and last_unit is not None:
                        add_sums(*last_unit)
                    if prep:
                        t = NQ * (h - H // 2) + k
                        if t > 0:
                            take_mask(c + 1, t - 1)
                        cast_adj(c + 1, t)
                    pair(c, h, k)
                    if epilogue and h == 0:
                        if k == 0:
                            take_mask(c, NB - 1)
                        if k == 1:
                            divide(c - 1)
                        if k == 3:
                            finish_sum(c - 1)
                    if epilogue and h == 1 and k == 0:
                        shifts(c - 1)

            unit(0, 0, False, False, None)
            unit(0, 1, False, False, (0, 0))
            with dve.Fori(0, NB - 1) as c:
                for h in range(H // 2, H):
                    unit(c, h, True, False, (c, h - 1))
                unit(c + 1, 0, False, True, (c, H - 1))
                unit(c + 1, 1, False, True, (c + 1, 0))
            for h in range(H // 2, H):
                unit(NB - 1, h, False, False, (NB - 1, h - 1))
            add_sums(NB - 1, H - 1)
            divide(NB - 1)
            finish_sum(NB - 1)
            shifts(NB - 1)


_INS = ["x", "adj", "L0_gnn_W", "L0_gnn_a_l", "L0_gnn_a_r"]


def kernel(**inputs):
    import numpy as np
    import concourse.bacc as bacc
    from concourse import mybir
    from concourse.bass_utils import run_bass_kernel_spmd

    nc = bacc.Bacc("TRN2", target_bir_lowering=False, num_devices=1, dynamic_dma_scratch_size=1024)
    arrays, args = {}, []
    for name in _INS:
        a = np.ascontiguousarray(inputs[name])
        arrays[f"in_{name}"] = a
        args.append(nc.dram_tensor(f"in_{name}", a.shape, mybir.dt.from_np(a.dtype), kind="ExternalInput").ap())
    n, d = inputs["x"].shape
    heads = inputs["L0_gnn_a_l"].shape[0]
    sl_rows = nc.dram_tensor("sl_rows", (heads, n), mybir.dt.float32, kind="Internal").ap()
    out = nc.dram_tensor("out", (n, d), mybir.dt.float32, kind="ExternalOutput").ap()
    graph_attention(nc, *args, sl_rows, out)
    r = run_bass_kernel_spmd(nc, [arrays], core_ids=[0])
    return r.results[0]["out"]
```

```python
def graph_attention(nc, x, adj, w, a_l, a_r, sl_rows, out):
    from contextlib import ExitStack
    from concourse import mybir

    dt, ALU, ACT = mybir.dt, mybir.AluOpType, mybir.ActivationFunctionType
    AX = mybir.AxisListType
    F32, F16, I32, U32, U8, I8, F8 = dt.float32, dt.float16, dt.int32, dt.uint32, dt.uint8, dt.int8, dt.float8e4

    P = 128
    N, D = x.shape
    H, DK = a_l.shape
    SUB = 4
    BLK = SUB * P
    NB = N // BLK
    KT = D // P
    DK1 = DK + 1
    PW = 2 * DK1
    WX = D + 2 * H
    QB = 2
    NQ = NB // QB
    WORDS = QB * BLK
    SHARE = ((7, 7, 7, 7), (7, 7, 7, 6), (6, 6, 6, 6), (6, 6, 6, 6))
    SHARE_LAST = ((6, 6, 6, 6), (6, 6, 6, 6), (5, 5, 5, 5), (5, 5, 6, 6))
    K_SCALE, K_ADD = 2, 3
    LATE_SCALE = {(2, 1): (0, 0), (3, 0): (0, 1), (3, 3): (0, 2)}
    LATE_ADD = {(2, 2): (0, 0), (3, 1): (0, 1), (3, 3): (0, 2)}
    AT_DIVIDE, AT_EXP, AT_FINISH, AT_SHIFTS, AT_NORM, AT_STORE = 3, 4, 4, 5, 7, 7
    POOL_HEADS = 3
    ALL, FIRST, LAST = (0, H), (0, H - 1), (H - 1, H)
    BIT = 0x20
    EDGE, CODE0 = 0x01010101, 0x40
    WIDE = 2.0 ** 13
    WIDE1 = 2.0 ** 14
    TINY = 1e-30
    EPS = 1e-5

    ctx = ExitStack()
    with ctx:
        def sb(name, shape, t):
            return ctx.enter_context(nc.sbuf_tensor(name, shape, t))

        def pb(name, shape, t):
            return ctx.enter_context(nc.psum_tensor(name, shape, t))

        def sem(name):
            return ctx.enter_context(nc.semaphore(name))

        ident = sb("ident", [P, P], F32)
        own = sb("own", [P, SUB, P], U32)
        ones = sb("ones", [H + 1, P], F32)
        half = sb("half", [P, SUB], F32)
        wext = sb("wext", [P, KT, WX], F32)
        slr = sb("slr", [P, NB, SUB, 2 * H], F32)
        nsr = sb("nsr", [P, NB, SUB, H], F32)
        cn = sb("cn", [P, NB, SUB, H], F32)
        rtop = sb("rtop", [P, NB, H], F32)
        below = sb("below", [P, NB, SUB, H], F32)
        near = sb("near", [P, NB, 2, SUB, H], F32)
        drop = sb("drop", [P, NB, H], F32)
        far = sb("far", [P, 2, NB, H], F32)
        wmax = sb("wmax", [P, NB], F32)
        peak = sb("peak", [P, H + 1], F32)
        high = sb("high", [H + 1, 1], F32)
        top = sb("top", [H + 1, H + 1], F32)
        smax = sb("smax", [P, H + 1], F32)
        wtop = sb("wtop", [P, 4], F32)
        slb = sb("slb", [P, H, BLK], F32)
        SLOT = SUB * H * PW
        store_parts = sb("store_parts", [P, (NB + 1) * SLOT], F32)
        scratch = sb("scratch", [P, SLOT], F32)
        parts = store_parts[:, 0:NB * SLOT].bitcast(F16).rearrange("p (m s h i e) -> p m s h i e", s=SUB, h=H, i=2, e=PW)

        def products(q):
            place = store_parts[:, (q + 2) * SLOT:(q + 3) * SLOT] if q + 2 <= NB else scratch[:]
            return place.rearrange("p (i s h e) -> p i s h e", i=2, s=SUB, h=H)

        sgn = sb("sgn", [P, NQ, WORDS], U32)
        bits = sb("bits", [P, NQ, 2, WORDS], U32)
        pairs = [(bits[:, k, 0], bits[:, k, 1]) for k in range(NQ)]

        def x_slot(q):
            return bits[:, q // 2, q % 2].bitcast(F32).rearrange("p (s d) -> p s d", s=SUB)

        adj_in = sb("adj_in", [P, 2, SUB, BLK], I32)
        adj_by = sb("adj_by", [P, 2, SUB * BLK], U8)
        mask = sb("mask", [P, 2, NB, BLK], U32)
        spare = mask[:, 1].rearrange("p q n -> p (q n)").bitcast(F32)
        o_rows = 2 * KT * BLK
        xt = spare[:, 0:o_rows].rearrange("p (s k n) -> p s k n", s=2, k=KT)
        rows = spare[0:H, o_rows:o_rows + 2 * BLK].rearrange("p (s n) -> p s n", s=2)
        aw = spare[:, o_rows + 2 * BLK:o_rows + 2 * BLK + 2 * D].rearrange("p (i d) -> p i d", i=2)
        xin = sb("xin", [P, SUB, D], F32)
        o_td, o_ts = SUB * H * DK1, SUB * H * DK1 + SUB * PW
        comb = scratch[:, 0:o_td].rearrange("p (s h e) -> p s h e", s=SUB, h=H)
        td = scratch[:, o_td:o_ts].rearrange("p (s e) -> p s e", s=SUB)
        ts = scratch[:, o_ts:o_ts + SUB * PW].rearrange("p (s e) -> p s e", s=SUB)
        den = sb("den", [P, 2, SUB, H], F32)
        y1 = sb("y1", [P, SUB, D], F32)
        y2 = sb("y2", [P, SUB, D], F32)
        stats = sb("stats", [P, SUB, 6], F32)
        mv = sb("mv", [P, SUB, 2], F32)
        var = sb("var", [P, SUB], F32)
        rstd = sb("rstd", [P, SUB], F32)
        shift = sb("shift", [P, SUB], F32)
        wh = [t[:].rearrange("p s (h d) -> p s h d", h=H) for t in (y1, y2)]

        acc = pb("acc", [P, 6, 512], F32)
        rb = acc[:, SUB:6, :]
        tb = pb("tb", [P, 2, 512], F32)

        def sums(h, s, i):
            g = SUB * i + s
            return 3 * (h % 2) + g // 3, PW * (g % 3)

        w_loaded, a_loaded = sem("w_loaded"), sem("a_loaded")
        x_loaded = [sem(f"x_loaded{q}") for q in range(NB)]
        adj_loaded = [sem(f"adj_loaded{i}") for i in range(2)]
        rows_stored = [sem(f"rows_stored{i}") for i in range(2)]
        sl_loaded = [sem(f"sl_loaded{h}") for h in range(H)]
        res_loaded, out_stored = sem("res_loaded"), sem("out_stored")
        consts_ready, wext_ready = sem("consts_ready"), sem("wext_ready")
        x_turned, xt_act, xt_dve = sem("x_turned"), sem("xt_act"), sem("xt_dve")
        wh_done, wh_copied, slr_copied = sem("wh_done"), sem("wh_copied"), sem("slr_copied")
        rtop_ready, below_ready, near_ready = sem("rtop_ready"), sem("below_ready"), sem("near_ready")
        product_done, wmax_ready = sem("product_done"), sem("wmax_ready")
        rows_turned, rows_copied, top_ready = sem("rows_turned"), sem("rows_copied"), sem("top_ready")
        peak_ready, peak_turned, smax_done = sem("peak_ready"), sem("peak_turned"), sem("smax_done")
        smax_copied, aggr_begun = sem("smax_copied"), sem("aggr_begun")
        drop_ready, far_ready, factors_ready = sem("drop_ready"), sem("far_ready"), sem("factors_ready")
        carg_ready, cn_ready = sem("carg_ready"), sem("cn_ready")
        head_act, head_pool, parts_ready = sem("head_act"), sem("head_pool"), sem("parts_ready")
        own_ready, bytes_ready, mask_turned, mask_ready = sem("own_ready"), sem("bytes_ready"), sem("mask_turned"), sem("mask_ready")
        own_added = sem("own_added")
        cmp_act, cmp_dve, pair_ready, quarter_done = sem("cmp_act"), sem("cmp_dve"), sem("pair_ready"), sem("quarter_done")
        quarter_begun = sem("quarter_begun")
        d_scaled, acc_free = sem("d_scaled"), sem("acc_free")
        comb_ready, den_ready, elu_ready, stats_ready = sem("comb_ready"), sem("den_ready"), sem("elu_ready"), sem("stats_ready")
        exp_part, sum_done, var_ready = sem("exp_part"), sem("sum_done"), sem("var_ready")
        rstd_ready, shift_ready, norm_done = sem("rstd_ready"), sem("shift_ready"), sem("norm_done")
        dve_order, pool_order = sem("dve_order"), sem("pool_order")

        assert NB == H // 2 * NQ

        def share(c, h, k):
            return (SHARE_LAST if isinstance(c, int) and c == NB - 1 else SHARE)[h][k]

        def sums_of(c, h, k, usual, late):
            if isinstance(c, int) and c == 0:
                return late.get((h, k))
            last_unit = (c, h - 1) if h > 0 else (c - 1, H - 1)
            return last_unit if k == usual else None

        def pool_heads(q):
            return H // 2 if q == 0 else POOL_HEADS

        block = ctx.enter_context(nc.Block())

        @block.sync
        def _(sp):
            def load_adj(c, q):
                if isinstance(c, int):
                    src = adj[c * BLK:(c + 1) * BLK, q * BLK:(q + 1) * BLK]
                else:
                    src = adj.rearrange("(c r) m -> c r m", r=BLK)[c, :, q * BLK:(q + 1) * BLK]
                if not isinstance(c, int) or NB * c + q >= 2:
                    sp.wait_ge(bytes_ready, NB * c + (q - 1))
                sp.dma_start(adj_in[:, q % 2], src.rearrange("(p s) m -> p s m", s=SUB)).then_inc(adj_loaded[q % 2], 16)

            def load_sl(c, h):
                if not isinstance(c, int) or c >= 1:
                    sp.wait_ge(cmp_act, 4 * H * (c - 1) + (4 * h + 4))
                    sp.wait_ge(cmp_dve, 4 * H * (c - 1) + (4 * h + 4))
                src = sl_rows.rearrange("h (c n) -> c h n", n=BLK)[c, h:h + 1, :]
                sp.dma_start(slb[:, h, :], src.to_broadcast([P, BLK])).then_inc(sl_loaded[h], 16)

            def load_res(c):
                src = x.rearrange("(c p s) d -> c p s d", p=P, s=SUB)[c]
                sp.dma_start(xin[:], src).then_inc(res_loaded, 16)

            sp.dma_start(wext[:, :, 0:D], w.rearrange("(k p) d -> p k d", p=P)).then_inc(w_loaded, 16)
            for i, a in enumerate((a_l, a_r)):
                sp.dma_start(aw[:, i, :], a.rearrange("h d -> (h d)").unsqueeze(0).to_broadcast([P, D])).then_inc(a_loaded, 16)
            def load_x(q):
                sp.dma_start(x_slot(q), x[q * BLK:(q + 1) * BLK, :].rearrange("(p s) d -> p s d", s=SUB)).then_inc(x_loaded[q], 16)

            load_x(0)
            load_x(1)
            load_adj(0, 0)
            load_adj(0, 1)
            load_x(2)
            load_x(3)
            for q in range(NB):
                load_adj(*divmod(q + 2, NB))
                if q + 4 < NB:
                    load_x(q + 4)
                sp.wait_ge(rows_copied, q + 1)
                sp.dma_start(sl_rows[:, q * BLK:(q + 1) * BLK], rows[:, q % 2, :]).then_inc(rows_stored[q % 2], 16)
                if q == 0:
                    sp.wait_ge(rows_stored[0], 16)
                    for h in range(H):
                        load_sl(0, h)
            for i in range(2):
                sp.wait_ge(rows_stored[i], 16 * (NB // 2))
            load_res(0)

            def during(c, more):
                first = isinstance(c, int) and c == 0
                last = isinstance(c, int) and c == NB - 1
                if not last:
                    load_adj(c + 1, 2)
                    load_adj(c + 1, 3)
                if not first:
                    load_sl(c, 2)
                    load_sl(c, 3)
                if not last:
                    load_adj(c + 1, 4)
                if not first:
                    sp.wait_ge(sum_done, c)
                    load_res(c)
                if not last:
                    load_adj(c + 1, 5)
                    load_sl(c + 1, 0)
                    load_adj(c + 1, 6)
                    load_adj(c + 1, 7)
                    load_sl(c + 1, 1)
                if more:
                    load_adj(c + 2, 0)
                    load_adj(c + 2, 1)

            during(0, True)
            with sp.Fori(1, NB - 2) as c:
                during(c, True)
            during(NB - 2, False)
            during(NB - 1, False)

        @block.gpsimd
        def _(pool):
            links = [0]

            def link(ins):
                links[0] += 1
                ins.then_inc(pool_order, 1)
                pool.wait_ge(pool_order, links[0])

            link(nc.gpsimd.memset(ident[:], 0.0))
            nc.gpsimd.affine_select(out=ident[:], in_=ident[:], compare_op=ALU.not_equal, fill=1.0, base=0,
                                    pattern=[[-1, P]], channel_multiplier=1).then_inc(consts_ready, 1)
            nc.gpsimd.memset(ones[:], 1.0).then_inc(consts_ready, 1)
            nc.gpsimd.memset(half[:], -0.5)
            pool.sem_inc(out_stored, 16)
            link(nc.gpsimd.memset(own[:], 0))
            for s in range(SUB):
                last = nc.gpsimd.affine_select(out=own[:, s].bitcast(I32), in_=own[:, s].bitcast(I32), compare_op=ALU.not_equal,
                                               fill=float(BIT << (8 * s)), base=0, pattern=[[-1, P]], channel_multiplier=1)
            last.then_inc(own_ready, 1)

            def inverse_root(c):
                pool.wait_ge(var_ready, c + 1)
                nc.gpsimd.tensor_tensor(rstd[:], var[:], half[:], ALU.pow).then_inc(rstd_ready, 1)

            for q in range(NB):
                pool.wait_ge(wh_copied, q + 1)
                pool.wait_ge(near_ready, q + 1)
                for i in range(2):
                    last = nc.gpsimd.tensor_tensor(products(q)[:, i, :, :, 0:DK], wh[q % 2],
                                                   near[:, q, i].unsqueeze(3).to_broadcast([P, SUB, H, DK]), ALU.mult)
                last.then_inc(product_done, 1)
            pool.wait_ge(factors_ready, 1)
            for q in range(NB):
                if q >= 2:
                    pool.wait_ge(parts_ready, q - 1)
                for h in range(pool_heads(q)):
                    last = nc.gpsimd.tensor_scalar(parts[:, q, :, h, 1, 0:DK1], products(q)[:, 1, :, h, :],
                                                   far[:, 1, q, h:h + 1], None, ALU.mult)
                last.then_inc(head_pool, 1)
            with pool.Fori(0, NB) as c:
                inverse_root(c)

        @block.tensor
        def _(pe):
            def turn_mask(c, q):
                pe.wait_ge(bytes_ready, NB * c + (q + 1))
                start = isinstance(c, int) and c == 0
                if not start:
                    pe.wait_ge(mask_ready, NB * c + (q - 1))
                elif q >= 1:
                    pe.wait_ge(mask_ready, q)
                bank = rb[:, 1, :] if start else tb[:, q % 2, :]
                by = adj_by[:, q % 2, :].bitcast(F32).rearrange("p (s w) -> p s w", s=SUB)
                for s in range(SUB):
                    last = nc.tensor.transpose(bank[:, s * P:(s + 1) * P], by[:, s, :], ident[:])
                last.then_inc(mask_turned, 1)

            def unit(c, h, prep):
                u = H * c + h
                for k in range(NQ):
                    if prep and k % 2 == 0:
                        turn_mask(c + 1, (NQ * h + k) // 2)
                    pe.wait_ge(pair_ready, NQ * u + (k + 1))
                    if isinstance(c, int) and u == 0:
                        pe.wait_ge(parts_ready, QB * (k + 1))
                    by = [m.bitcast(F8).rearrange("p (q s j b) -> p q s j b", q=QB, s=SUB, b=SUB)
                          for m in pairs[k]]
                    if k == 0 and (not isinstance(c, int) or u >= 2):
                        pe.wait_ge(acc_free, u - 1)
                    pe.sem_inc(quarter_begun, 1)
                    begun = set()
                    for s in range(SUB):
                        for q in range(QB):
                            for b in range(SUB):
                                for i in range(2):
                                    bank, col = sums(h, s, i)
                                    first = k == 0 and bank not in begun
                                    begun.add(bank)
                                    final = k == NQ - 1 and q == QB - 1 and b == SUB - 1
                                    last = nc.tensor.matmul(acc[:, bank, col:col + PW], by[i][:, q, s, :, b],
                                                            parts[:, QB * k + q, b, h, i, :],
                                                            start=first, stop=final, skip_group_check=True)
                    last.then_inc(quarter_done, 1)

            def turn_x(q):
                pe.wait_ge(x_loaded[q], 16)
                if q >= 1:
                    pe.wait_ge(xt_act, q)
                    pe.wait_ge(xt_dve, q)
                for kk in range(KT):
                    for s in range(SUB):
                        last = nc.tensor.transpose(tb[:, kk, s * P:(s + 1) * P], x_slot(q)[:, s, kk * P:(kk + 1) * P], ident[:])
                last.then_inc(x_turned, 1)

            def turn_rows(q):
                pe.wait_ge(slr_copied, q + 1)
                if q >= 1:
                    pe.wait_ge(rows_copied, q)
                for s in range(SUB):
                    last = nc.tensor.transpose(rb[0:H, 0, s * P:(s + 1) * P], slr[:, q, s, 0:H], ident[:])
                last.then_inc(rows_turned, 1)

            pe.wait_ge(consts_ready, 1)
            turn_x(0)
            for q in range(NB):
                if q + 1 < NB:
                    turn_x(q + 1)
                pe.wait_ge(xt_act, q + 1)
                pe.wait_ge(xt_dve, q + 1)
                if q == 0:
                    pe.wait_ge(wext_ready, 1)
                else:
                    pe.wait_ge(wh_copied, q)
                for s in range(SUB):
                    for kk in range(KT):
                        last = nc.tensor.matmul(acc[:, s, 0:WX], xt[:, q % 2, kk, s * P:(s + 1) * P], wext[:, kk, :],
                                                start=kk == 0, stop=kk == KT - 1)
                last.then_inc(wh_done, 1)
                turn_mask(0, q)
                turn_rows(q)
            pe.wait_ge(peak_ready, 1)
            pe.wait_ge(rows_copied, NB)
            pe.wait_ge(mask_ready, NB)
            nc.tensor.transpose(rb[0:H + 1, 1, 0:P], peak[:], ident[:]).then_inc(peak_turned, 1)
            pe.wait_ge(top_ready, 1)
            pe.wait_ge(consts_ready, 2)
            nc.tensor.matmul(rb[:, 0, 0:H + 1], ones[:, :], top[:], start=True, stop=True).then_inc(smax_done, 1)
            pe.wait_ge(wh_copied, NB)
            pe.wait_ge(smax_copied, 1)
            for h in range(H):
                unit(0, h, True)
            with pe.Fori(1, NB - 1) as c:
                for h in range(H):
                    unit(c, h, True)
            for h in range(H):
                unit(NB - 1, h, False)

        @block.scalar
        def _(act):
            def compare_block(h, q):
                k = q // QB
                if q == 0:
                    act.wait_ge(sl_loaded[h], 16)
                if h >= 1 and q % QB == 0:
                    act.wait_ge(pair_ready, NQ * (h - 1) + k + 1)
                to = sgn[:, k, :].bitcast(I8).rearrange("p (q n b) -> p q n b", q=QB, b=SUB)
                for b in range(SUB):
                    last = nc.scalar.activation(to[:, q % QB, :, b], slb[:, h, :], ACT.Sign,
                                                bias=slr[:, q, b, H + h:H + h + 1])
                if q % QB == QB - 1:
                    last.then_inc(cmp_act, 1)

            def compare(c, h, k, between=None):
                g = NQ * (H * c + h) + k
                if k == 0:
                    act.wait_ge(sl_loaded[h], 16 * c + 16)
                act.wait_ge(pair_ready, g - (NQ - 1))
                to = sgn[:, k, :].bitcast(I8).rearrange("p (q n b) -> p q n b", q=QB, b=SUB)
                for i in range(share(c, h, k)):
                    q, b = i // SUB, i % SUB
                    last = nc.scalar.activation(to[:, q, :, b], slb[:, h, :], ACT.Sign,
                                                bias=slr[:, QB * k + q, b, H + h:H + h + 1])
                    if i == share(c, h, k) - 1:
                        last.then_inc(cmp_act, 1)
                    if between is not None and i >= share(c, h, k) - SUB:
                        scale_d(*between, i - (share(c, h, k) - SUB))

            def scale_d(c, h, s):
                u = H * c + h
                if s == 0:
                    act.wait_ge(quarter_done, NQ * u + NQ)
                    if not isinstance(c, int) or u >= 1:
                        act.wait_ge(acc_free, u)
                bank, col = sums(h, s, 1)
                ins = nc.scalar.activation(td[:, s, :], acc[:, bank, col:col + PW], ACT.Copy, scale=cn[:, c, s, h:h + 1])
                if s == SUB - 1:
                    ins.then_inc(d_scaled, 1)

            def exponential(c, step, heads=ALL):
                cols = slice(heads[0] * DK, heads[1] * DK)
                act.wait_ge(den_ready, 4 * step + 4)
                act.wait_ge(out_stored, 16 * c + 16)
                nc.scalar.activation(y2[:, :, cols], y1[:, :, cols], ACT.Exp).then_inc(exp_part, 1)

            def normalize(c):
                act.wait_ge(shift_ready, c + 1)
                for s in range(SUB):
                    last = nc.scalar.activation(y2[:, s, :], y1[:, s, :], ACT.Identity, bias=shift[:, s:s + 1],
                                                scale=rstd[:, s:s + 1])
                last.then_inc(norm_done, 1)

            def store(c):
                act.wait_ge(norm_done, c + 1)
                act.dma_start(out.rearrange("(c p s) d -> c p s d", p=P, s=SUB)[c], y2[:]).then_inc(out_stored, 16)

            def take_x(q):
                act.wait_ge(x_turned, q + 1)
                if q >= 2:
                    act.wait_ge(wh_done, q - 1)
                nc.scalar.copy(xt[:, q % 2, 0, :], tb[:, 0, :]).then_inc(xt_act, 1)

            def take_rows(q):
                act.wait_ge(rows_turned, q + 1)
                if q >= 2:
                    act.wait_ge(rows_stored[q % 2], 16 * (q // 2))
                nc.scalar.copy(rows[:, q % 2, :], rb[0:H, 0, :]).then_inc(rows_copied, 1)

            take_x(0)
            for q in range(NB):
                if q + 1 < NB:
                    take_x(q + 1)
                act.wait_ge(slr_copied, q + 1)
                if q >= 2:
                    act.wait_ge(product_done, q - 1)
                    act.wait_ge(wmax_ready, q - 1)
                nc.scalar.copy(wh[q % 2], acc[:, 0:SUB, 0:D].rearrange("p s (h d) -> p s h d", h=H)).then_inc(wh_copied, 1)
                act.wait_ge(below_ready, q + 1)
                nc.scalar.activation(near[:, q, 0], below[:, q], ACT.Exp)
                nc.scalar.activation(near[:, q, 1], below[:, q], ACT.Exp, scale=0.2).then_inc(near_ready, 1)
                take_rows(q)
                if q == 2:
                    compare_block(0, 0)
                if q >= 2:
                    compare_block(0, q - 1)
            compare_block(0, NB - 1)
            act.wait_ge(drop_ready, 1)
            nc.scalar.activation(far[:, 0], drop[:], ACT.Exp)
            nc.scalar.activation(far[:, 1], drop[:], ACT.Exp, scale=0.2).then_inc(far_ready, 1)
            act.wait_ge(carg_ready, 1)
            nc.scalar.activation(cn[:], cn[:], ACT.Exp, scale=-0.8).then_inc(cn_ready, 1)
            act.wait_ge(factors_ready, 1)
            for q in range(NB):
                if q >= 2:
                    act.wait_ge(parts_ready, q - 1)
                for i, h in [(0, h) for h in range(H)] + [(1, h) for h in range(pool_heads(q), H)]:
                    last = nc.scalar.activation(parts[:, q, :, h, i, 0:DK1], products(q)[:, i, :, h, :], ACT.Copy,
                                                scale=far[:, i, q, h:h + 1])
                last.then_inc(head_act, 1)
                compare_block(1, q)

            def unit(c, h):
                epilogue = not isinstance(c, int) or c >= 1
                for k in range(NQ):
                    compare(c, h, k, sums_of(c, h, k, K_SCALE, LATE_SCALE))
                    if epilogue and NQ * h + k == AT_EXP:
                        exponential(c - 1, c - 1)
                    if epilogue and NQ * h + k == AT_NORM:
                        normalize(c - 1)
                    if epilogue and NQ * h + k == AT_STORE:
                        store(c - 1)

            act.wait_ge(cn_ready, 1)
            for h in range(H // 2, H):
                unit(0, h)
            with act.Fori(1, NB - 1) as c:
                for h in range(H):
                    unit(c, h)
            for h in range(H):
                unit(NB - 1, h)
            exponential(NB - 1, NB - 1, FIRST)
            for s in range(SUB):
                scale_d(NB - 1, H - 1, s)
            exponential(NB - 1, NB, LAST)
            normalize(NB - 1)
            store(NB - 1)
            act.wait_ge(out_stored, 16 * NB + 16)

        @block.vector
        def _(dve):
            links = [0]

            def link(ins):
                links[0] += 1
                ins.then_inc(dve_order, 1)
                dve.wait_ge(dve_order, links[0])

            def cast_adj(c, q):
                dve.wait_ge(adj_loaded[q % 2], 16 * (4 * c + (q // 2 + 1)))
                if not isinstance(c, int) or NB * c + q >= 2:
                    dve.wait_ge(mask_turned, NB * c + (q - 1))
                nc.vector.tensor_scalar(adj_by[:, q % 2, :], adj_in[:, q % 2].rearrange("p s m -> p (s m)"), 0.0, float(CODE0),
                                        ALU.is_gt, ALU.add).then_inc(bytes_ready, 1)

            def take_mask(c, q):
                dve.wait_ge(mask_turned, NB * c + (q + 1))
                bank = rb[:, 1, :] if isinstance(c, int) and c == 0 else tb[:, q % 2, :]
                nc.vector.tensor_scalar(mask[:, c & 1, q, :], bank.bitcast(U32), EDGE, 5,
                                        ALU.bitwise_and, ALU.logical_shift_left).then_inc(mask_ready, 1)

            def add_own(c):
                dve.wait_ge(mask_ready, NB * c + (c + 1))
                diagonal = mask[:, c & 1, c, :]
                nc.vector.tensor_tensor(diagonal, diagonal, own[:].rearrange("p s n -> p (s n)"), ALU.bitwise_or).then_inc(own_added, 1)
                dve.wait_ge(own_added, c + 1)

            def compare(c, h, k):
                if k == 0:
                    dve.wait_ge(sl_loaded[h], 16 * c + 16)
                to = sgn[:, k, :].bitcast(U8).rearrange("p (q n b) -> p q n b", q=QB, b=SUB)
                for i in range(share(c, h, k), QB * SUB):
                    q, b = i // SUB, i % SUB
                    last = nc.vector.tensor_scalar(to[:, q, :, b], slb[:, h, :], nsr[:, QB * k + q, b, h:h + 1],
                                                   float(BIT), ALU.is_le, ALU.mult)
                last.then_inc(cmp_dve, 1)

            def pair(c, h, k):
                g = NQ * (H * c + h) + k
                dve.wait_ge(cmp_act, g + 1)
                dve.wait_ge(cmp_dve, g + 1)
                dve.wait_ge(mask_ready, NB * c + QB * (k + 1))
                if not isinstance(c, int) or g >= NQ:
                    dve.wait_ge(quarter_done, g - (NQ - 1))
                m = mask[:, c & 1, QB * k:QB * (k + 1), :].rearrange("p q n -> p (q n)")
                nc.vector.tensor_tensor(pairs[k][1], sgn[:, k, :], m, ALU.bitwise_and)
                nc.vector.scalar_tensor_tensor(out=pairs[k][0], in0=sgn[:, k, :], scalar=BIT * EDGE, in1=m,
                                               op0=ALU.bitwise_xor, op1=ALU.bitwise_and).then_inc(pair_ready, 1)

            def add_sums(c, h):
                u = H * c + h
                dve.wait_ge(d_scaled, u + 1)
                bank, _ = sums(h, 0, 0)
                three = acc[:, bank, 0:3 * PW].rearrange("p (s n) -> p s n", s=3)
                nc.vector.tensor_tensor(ts[:, 0:3, :], three, td[:, 0:3, :], ALU.add)
                nc.vector.tensor_tensor(ts[:, 3, :], acc[:, bank + 1, 0:PW], td[:, 3, :], ALU.add).then_inc(acc_free, 1)
                dve.wait_ge(acc_free, u + 1)
                nc.vector.tensor_tensor(comb[:, :, h, :], ts[:, :, 0:DK1], ts[:, :, DK1:PW], ALU.add).then_inc(comb_ready, 1)

            def divide(c, step, heads=ALL):
                some = slice(*heads)
                cols = slice(heads[0] * DK, heads[1] * DK)
                dve.wait_ge(comb_ready, H * c + heads[1])
                nc.vector.tensor_scalar(den[:, 0, :, some], comb[:, :, some, DK], TINY, None, ALU.max).then_inc(den_ready, 1)
                dve.wait_ge(den_ready, 4 * step + 1)
                nc.vector.reciprocal(den[:, 1, :, some], den[:, 0, :, some]).then_inc(den_ready, 1)
                dve.wait_ge(den_ready, 4 * step + 2)
                nc.vector.tensor_scalar(den[:, 0, :, some], den[:, 1, :, some], wtop[:, 2:3], None, ALU.mult).then_inc(den_ready, 1)
                dve.wait_ge(den_ready, 4 * step + 3)
                nc.vector.tensor_tensor(y1[:, :, cols].rearrange("p s (h d) -> p s h d", d=DK), comb[:, :, some, 0:DK],
                                        den[:, 0, :, some].unsqueeze(3).to_broadcast([P, SUB, heads[1] - heads[0], DK]),
                                        ALU.mult).then_inc(den_ready, 1)

            def add_residual(c, step, heads=ALL):
                cols = slice(heads[0] * DK, heads[1] * DK)
                dve.wait_ge(exp_part, step + 1)
                dve.wait_ge(res_loaded, 16 * c + 16)
                nc.vector.scalar_tensor_tensor(out=y2[:, :, cols], in0=y2[:, :, cols], scalar=1.0, in1=xin[:, :, cols],
                                               op0=ALU.min, op1=ALU.add).then_inc(elu_ready, 1)
                dve.wait_ge(elu_ready, step + 1)
                nc.vector.scalar_tensor_tensor(out=y1[:, :, cols], in0=y1[:, :, cols], scalar=0.0, in1=y2[:, :, cols],
                                               op0=ALU.max, op1=ALU.add).then_inc(sum_done, 1)

            def moments(c, step):
                dve.wait_ge(sum_done, step + 1)
                for s in range(SUB):
                    last = nc.vector.bn_stats(stats[:, s, :], y1[:, s, :])
                last.then_inc(stats_ready, 1)
                dve.wait_ge(stats_ready, 2 * c + 1)
                dve.sem_inc(aggr_begun, 1)
                for s in range(SUB):
                    last = nc.vector.bn_aggr(mv[:, s, :], stats[:, s, :])
                last.then_inc(stats_ready, 1)
                dve.wait_ge(stats_ready, 2 * c + 2)
                nc.vector.tensor_scalar(var[:], mv[:, :, 1], EPS, None, ALU.add).then_inc(var_ready, 1)

            def shifts(c):
                dve.wait_ge(rstd_ready, c + 1)
                nc.vector.scalar_tensor_tensor(out=shift[:], in0=mv[:, :, 0], scalar=-1.0, in1=rstd[:],
                                               op0=ALU.mult, op1=ALU.mult).then_inc(shift_ready, 1)

            dve.wait_ge(w_loaded, 16)
            dve.wait_ge(a_loaded, 32)
            for i in range(2):
                for kk in range(KT):
                    prod = y1[:, 2 * i + kk, :]
                    last = nc.vector.tensor_tensor(prod, wext[:, kk, 0:D], aw[:, i, :], ALU.mult)
            link(last)
            for i in range(2):
                for kk in range(KT):
                    prod = y1[:, 2 * i + kk, :].rearrange("p (h d) -> p h d", h=H)
                    last = nc.vector.reduce_sum(wext[:, kk, D + i * H:D + (i + 1) * H], prod, AX.X)
            last.then_inc(wext_ready, 1)
            dve.sem_inc(cmp_dve, 2 * NQ)

            def take_x(q):
                dve.wait_ge(x_turned, q + 1)
                if q >= 2:
                    dve.wait_ge(wh_done, q - 1)
                nc.vector.tensor_copy(xt[:, q % 2, 1, :], tb[:, 1, :]).then_inc(xt_dve, 1)

            take_x(0)
            cast_adj(0, 0)
            for q in range(NB):
                if q + 1 < NB:
                    take_x(q + 1)
                dve.wait_ge(wh_done, q + 1)
                nc.vector.tensor_copy(slr[:, q], acc[:, 0:SUB, D:WX]).then_inc(slr_copied, 1)
                dve.wait_ge(slr_copied, q + 1)
                sr = slr[:, q, :, H:2 * H]
                nc.vector.tensor_reduce(out=rtop[:, q], in_=sr.rearrange("p s h -> p h s"), op=ALU.max, axis=AX.X).then_inc(rtop_ready, 1)
                dve.wait_ge(rtop_ready, q + 1)
                nc.vector.tensor_tensor(below[:, q], sr, rtop[:, q].unsqueeze(1).to_broadcast([P, SUB, H]),
                                        ALU.subtract).then_inc(below_ready, 1)
                take_mask(0, q)
                if q + 1 < NB:
                    cast_adj(0, q + 1)
                dve.wait_ge(wh_copied, q + 1)
                nc.vector.tensor_reduce(out=wmax[:, q:q + 1], in_=wh[q % 2].rearrange("p s h d -> p (s h d)"),
                                        op=ALU.max, axis=AX.X, apply_absolute_value=True).then_inc(wmax_ready, 1)
                if q == 3:
                    dve.wait_ge(own_ready, 1)
                    add_own(0)
                if q in (3, 5):
                    pair(0, 0, (q - 3) // 2)
            nc.vector.tensor_reduce(out=peak[:, 0:H], in_=rtop[:].rearrange("p q h -> p h q"), op=ALU.max, axis=AX.X)
            dve.wait_ge(wmax_ready, NB)
            nc.vector.tensor_reduce(out=peak[:, H:H + 1], in_=wmax[:], op=ALU.max, axis=AX.X).then_inc(peak_ready, 1)
            nc.vector.tensor_scalar(nsr[:], slr[:, :, :, H:2 * H], -1.0, None, ALU.mult)
            cast_adj(1, 0)
            dve.wait_ge(peak_turned, 1)
            link(nc.vector.tensor_reduce(out=high[:], in_=rb[0:H + 1, 1, 0:P], op=ALU.max, axis=AX.X))
            nc.vector.tensor_scalar(top[:], ident[0:H + 1, 0:H + 1], high[:], None, ALU.mult).then_inc(top_ready, 1)
            dve.wait_ge(smax_done, 1)
            last = nc.vector.tensor_copy(smax[:], rb[:, 0, 0:H + 1])
            last.then_inc(smax_copied, 1)
            dve.wait_ge(smax_copied, 1)
            nc.vector.tensor_tensor(drop[:], rtop[:], smax[:, 0:H].unsqueeze(1).to_broadcast([P, NB, H]),
                                    ALU.subtract).then_inc(drop_ready, 1)
            flat = lambda t: t.rearrange("p q s h -> p (q s) h")
            link(nc.vector.tensor_tensor(flat(cn[:]), flat(slr[:, :, :, 0:H]),
                                         smax[:, 0:H].unsqueeze(1).to_broadcast([P, NB * SUB, H]), ALU.add))
            nc.vector.tensor_scalar(cn[:], cn[:], 0.0, None, ALU.max).then_inc(carg_ready, 1)
            link(nc.vector.tensor_scalar(wtop[:, 0:1], smax[:, H:H + 1], TINY, None, ALU.max))
            link(nc.vector.reciprocal(wtop[:, 1:2], wtop[:, 0:1]))
            nc.vector.tensor_scalar(wtop[:, 2:3], wtop[:, 0:1], WIDE1 / WIDE, None, ALU.mult)
            link(nc.vector.tensor_scalar(wtop[:, 1:2], wtop[:, 1:2], WIDE, None, ALU.mult))
            link(nc.vector.reciprocal(wtop[:, 3:4], wtop[:, 1:2]))
            link(nc.vector.tensor_scalar(wtop[:, 3:4], wtop[:, 3:4], WIDE1, None, ALU.mult))
            dve.wait_ge(product_done, NB)
            group = lambda t: t.rearrange("p (m g e) -> p m g e", m=1 if t.shape[1] == SLOT else NB - 1, e=DK1)[:, :, :, DK]
            factor = wtop[:, 3:4]
            nc.vector.tensor_scalar(group(store_parts[:, 2 * SLOT:(NB + 1) * SLOT]),
                                    near[:, 0:NB - 1].rearrange("p q i s h -> p q (i s h)"), factor, None, ALU.mult)
            nc.vector.tensor_scalar(group(scratch[:]), near[:, NB - 1:NB].rearrange("p q i s h -> p q (i s h)"), factor, None, ALU.mult)
            dve.wait_ge(far_ready, 1)
            nc.vector.tensor_scalar(far[:], far[:], wtop[:, 1:2], None, ALU.mult).then_inc(factors_ready, 1)
            dve.wait_ge(factors_ready, 1)
            pair(0, 0, 2)
            for q in range(NB):
                dve.wait_ge(head_act, q + 1)
                dve.wait_ge(head_pool, q + 1)
                for i in range(2):
                    for h in range(H):
                        last = nc.vector.scalar_tensor_tensor(out=parts[:, q, :, h, i, DK1:PW], in0=products(q)[:, i, :, h, :],
                                                              scalar=far[:, i, q, h:h + 1], in1=parts[:, q, :, h, i, 0:DK1],
                                                              op0=ALU.mult, op1=ALU.subtract)
                last.then_inc(parts_ready, 1)
                if q == 1:
                    pair(0, 0, 3)
                    cast_adj(1, 1)
                if q == 3:
                    take_mask(1, 0)
                if q == 5:
                    cast_adj(1, 2)
                if q >= 3 and q % 2 == 1:
                    pair(0, 1, (q - 3) // 2)
            take_mask(1, 1)
            cast_adj(1, 3)
            pair(0, 1, NQ - 1)
            take_mask(1, 2)

            def unit(c, h, prep):
                epilogue = not isinstance(c, int) or c >= 1
                for k in range(NQ):
                    compare(c, h, k)
                    whole = sums_of(c, h, k, K_ADD, LATE_ADD)
                    if whole is not None:
                        add_sums(*whole)
                    t = (NQ * h + k) // 2
                    if k % 2 == 0 and prep:
                        cast_adj(c + 1, t)
                    if k % 2 == 1 and t == 0:
                        take_mask(c, NB - 1)
                    elif k % 2 == 1 and prep:
                        take_mask(c + 1, t - 1)
                    if h == 0 and k == (1 if isinstance(c, int) else 0):
                        add_own(c)
                    pair(c, h, k)
                    if epilogue and NQ * h + k == AT_DIVIDE:
                        divide(c - 1, c - 1)
                    if epilogue and NQ * h + k == AT_FINISH:
                        add_residual(c - 1, c - 1)
                        moments(c - 1, c - 1)
                    if epilogue and NQ * h + k == AT_SHIFTS:
                        shifts(c - 1)

            for h in range(H // 2, H):
                unit(0, h, True)
            with dve.Fori(1, NB - 1) as c:
                for h in range(H):
                    unit(c, h, True)
            for h in range(H):
                unit(NB - 1, h, False)
            divide(NB - 1, NB - 1, FIRST)
            add_residual(NB - 1, NB - 1, FIRST)
            add_sums(NB - 1, H - 1)
            divide(NB - 1, NB, LAST)
            add_residual(NB - 1, NB, LAST)
            moments(NB - 1, NB)
            shifts(NB - 1)


_INS = ["x", "adj", "L0_gnn_W", "L0_gnn_a_l", "L0_gnn_a_r"]


def kernel(**inputs):
    import numpy as np
    import concourse.bacc as bacc
    from concourse import mybir
    from concourse.bass_utils import run_bass_kernel_spmd

    nc = bacc.Bacc("TRN2", target_bir_lowering=False, num_devices=1, dynamic_dma_scratch_size=1024)
    arrays, args = {}, []
    for name in _INS:
        a = np.ascontiguousarray(inputs[name])
        arrays[f"in_{name}"] = a
        args.append(nc.dram_tensor(f"in_{name}", a.shape, mybir.dt.from_np(a.dtype), kind="ExternalInput").ap())
    n, d = inputs["x"].shape
    heads = inputs["L0_gnn_a_l"].shape[0]
    sl_rows = nc.dram_tensor("sl_rows", (heads, n), mybir.dt.float32, kind="Internal").ap()
    out = nc.dram_tensor("out", (n, d), mybir.dt.float32, kind="ExternalOutput").ap()
    graph_attention(nc, *args, sl_rows, out)
    r = run_bass_kernel_spmd(nc, [arrays], core_ids=[0])
    return r.results[0]["out"]
```
